# Optimizing a Trainium2 kernel written in Bass

```python
import numpy as np
import jax
import jax.numpy as jnp

def _softmax(x, axis=-1):
    return jax.nn.softmax(x, axis=axis)

def _gelu(x):
    return jax.nn.gelu(x, approximate=True)

def _silu(x):
    return jax.nn.silu(x)

def _sigmoid(x):
    return jax.nn.sigmoid(x)

def _layernorm(x, axis=-1, eps=1e-05):
    m = jnp.mean(x, axis=axis, keepdims=True)
    v = jnp.var(x, axis=axis, keepdims=True)
    return (x - m) / jnp.sqrt(v + eps)

def _scatter_add(tgt, idx, src, axis=0):
    return tgt.at[idx].add(src)

def _segment_sum(src, seg, n):
    return jax.ops.segment_sum(src, seg, n)
kernel_name = 'mk_adj_resnorm_d2_adj_r2_86b44a'

def setup_inputs(seed: int=0):
    np.random.seed(seed)
    _w = jnp.asarray

    def _rec_inputs():
        import jax
        import jax.numpy as jnp
        _gk = jax.random.key(seed)
        x = -9.806e-05 + 1 * jax.random.normal(jax.random.fold_in(_gk, 1), (8192, 64), jnp.float32)
        _a = jax.random.bernoulli(jax.random.fold_in(_gk, 2), 0.000244141, (8192, 8192))
        _a = jnp.logical_or(_a, jnp.swapaxes(_a, -1, -2))
        _a = jnp.logical_or(_a, jnp.eye(8192, dtype=bool))
        _af = _a.astype(jnp.float32)
        adj = _af
        return (x, adj)
    x, adj = _rec_inputs()

    def _L0_gnn_setup():
        import jax, jax.numpy as jnp
        import numpy as np
        N, D_IN, D_OUT = (4096, 64, 64)
        MAX_NEIGH = 100
        DECAY = 0.5
        key = jax.random.key(seed)
        k1, k2, k3, k4 = jax.random.split(key, 4)
        stdv = 1.0 / np.sqrt(D_OUT)
        inputs = {'input': jax.random.normal(k1, (N, D_IN), dtype=jnp.float32), 'adj': jax.random.randint(k2, (N, N), 0, 2).astype(jnp.float32), 'weight': jax.random.uniform(k3, (D_IN, D_OUT), minval=-stdv, maxval=stdv, dtype=jnp.float32), 'bias': jax.random.uniform(k4, (D_OUT,), minval=-stdv, maxval=stdv, dtype=jnp.float32)}
        return inputs
    _L0_gnn_all = _L0_gnn_setup()
    _L0_gnn_in = {k: v for k, v in _L0_gnn_all.items() if k in ('weight', 'bias')}
    del _L0_gnn_all

    def _L1_gnn_setup():
        import jax, jax.numpy as jnp
        import numpy as np
        N = 5000
        DIM = 64
        F_CONST = 1.0
        B_CONST = 0.1
        R_CONST = 0.01
        key = jax.random.key(seed)
        k1, k2 = jax.random.split(key)
        t = jnp.zeros((1,), dtype=jnp.float32)
        x = jax.random.uniform(k1, (N, DIM), dtype=jnp.float32)
        A = jax.random.uniform(k2, (N, N), dtype=jnp.float32)
        return {'t': t, 'x': x, 'A': A}
    _L1_gnn_all = _L1_gnn_setup()
    _L1_gnn_in = {k: v for k, v in _L1_gnn_all.items() if k in ('t',)}
    del _L1_gnn_all
    return {'x': x, 'adj': adj, 'L0_gnn_weight': _L0_gnn_in['weight'], 'L0_gnn_bias': _L0_gnn_in['bias'], 'L1_gnn_t': _L1_gnn_in['t']}

def reference(x, adj, L0_gnn_weight, L0_gnn_bias, L1_gnn_t):
    import jax
    import jax.numpy as jnp

    def _L0_gnn_ref(input, adj, weight, bias):
        import jax, jax.numpy as jnp
        import numpy as np
        N, D_IN, D_OUT = (4096, 64, 64)
        MAX_NEIGH = 100
        DECAY = 0.5
        support = input @ weight
        mask = (adj != 0).astype(support.dtype)
        rank = jnp.cumsum(mask, axis=1)
        deg = rank[:, -1:]
        k = jnp.minimum(deg, float(MAX_NEIGH))
        pos = rank - (deg - k)
        w = mask * jnp.where(pos > 0, DECAY ** (k - pos), 0.0)
        out = w @ support + bias
        return out

    def _L1_gnn_ref(t, x, A):
        import jax, jax.numpy as jnp
        import numpy as np
        N = 5000
        DIM = 64
        F_CONST = 1.0
        B_CONST = 0.1
        R_CONST = 0.01
        Ax = A @ x
        outer = R_CONST * jnp.sum(x * Ax, axis=1, keepdims=True)
        return F_CONST - B_CONST * x - outer
    x = _layernorm(x + _L0_gnn_ref(x, adj, L0_gnn_weight, L0_gnn_bias), axis=-1)
    x = _layernorm(x + _L1_gnn_ref(L1_gnn_t, x, adj), axis=-1)
    return x

_drawn_inputs = setup_inputs


def setup_inputs(seed=0):
    import zlib

    import numpy as np

    out = dict(_drawn_inputs(seed))
    spreads = {}
    factors = {}
    for name, (base, spread) in spreads.items():
        noise = np.random.default_rng([zlib.crc32(name.encode()), seed]).standard_normal(out[name].shape)
        drawn = base * np.exp(spread * noise) if base else spread * noise
        out[name] = jnp.asarray(drawn.astype(out[name].dtype))
    for name, factor in factors.items():
        out[name] = (out[name] * factor).astype(out[name].dtype)
    return out
```

```python
from contextlib import ExitStack

import concourse.bass as bass
from concourse import mybir

ALU = mybir.AluOpType
ACT = mybir.ActivationFunctionType
AXX = mybir.AxisListType.X
F32 = mybir.dt.float32
BF16 = mybir.dt.bfloat16
I16 = mybir.dt.int16

P = 128
MAX_NEIGH = 100
EPS = 1e-5
F_CONST, B_CONST, R_CONST = 1.0, 0.1, 0.01
WEIGHT_SHIFT = 2.0 ** (127 - MAX_NEIGH)
BF16_EXPONENT_STEP = 128.0


def adj_resnorm_kernel(nc, x, adj, weight, bias, out):
    N, D = x.shape
    NB = N // P
    TI = 8
    STRIP = TI * P
    NS = N // STRIP
    CJ = 512
    NQ = N // CJ
    TJ = CJ // P
    SLOTS = 4
    STEPS = SLOTS * TJ
    BODIES = NB // STEPS
    CHAINS = 2
    HALF = STRIP // CHAINS
    TH = HALF // P
    PIECES = 3 * D
    GRING = 4

    adj_v = adj.rearrange("(s t p) j -> s p t j", t=TI, p=P)
    x_v = x.rearrange("(b p) d -> p b d", p=P)
    out_v = out.rearrange("(s t p) d -> s p t d", t=TI, p=P)

    ctx = ExitStack()
    with ctx:
        def sb(name, shape, dt):
            return ctx.enter_context(nc.sbuf_tensor(name, shape, dt))

        def pb(name, shape, dt):
            return ctx.enter_context(nc.psum_tensor(name, shape, dt))

        def sem(name):
            return ctx.enter_context(nc.semaphore(name))

        A = [sb(f"A{k}", [P, TI, CJ], F32) for k in range(SLOTS)]
        A_high = [a[:, :, :].bitcast(BF16) for a in A]
        x_all = sb("x_all", [P, NB, D], F32)
        w_sb = sb("w_sb", [P, D], F32)
        bias_sb = sb("bias_sb", [P, D], F32)
        support = sb("support", [P, NB, PIECES], BF16)
        rest = sb("rest", [P, TI, D], F32)
        rest2 = sb("rest2", [P, TI, D], F32)
        x_group = sb("x_group", [P, TI, P], F32)
        x_groupT = sb("x_groupT", [P, STRIP], F32)
        xT = sb("xT", [P, N], F32)
        ident = sb("ident", [P, P], F32)
        ident_b = sb("ident_b", [P, P], BF16)
        count_w = sb("count_w", [P, P], BF16)
        carry_w = sb("carry_w", [P, P], BF16)
        zeros = sb("zeros", [P, 512], BF16)
        mask = [sb(f"mask{k}", [P, STRIP], BF16) for k in range(2)]
        wgt = [[sb(f"wgt{c}{k}", [P, HALF], BF16) for k in range(2)] for c in range(CHAINS)]
        strip_pad = sb("strip_pad", [P, TI, P], F32)
        strip = strip_pad[:, :, 0:D]
        square = sb("square", [P, TI, D], F32)
        junk = [sb(f"junk{k}", [P, CJ], BF16) for k in range(2)]
        part = sb("part", [P, TI, NQ], F32)
        col = [sb(f"col{k}", [P, TI], F32) for k in range(8)]

        acc = pb("acc", [P, GRING, 512], F32)
        acc_v = acc[:, :, 0:2 * PIECES].rearrange("p b (h c) -> p b h c", h=2)
        count = [pb(f"count{c}", [P, HALF], F32) for c in range(CHAINS)]
        tp = [pb(f"tp{k}", [P, STRIP], BF16) for k in range(2)]
        tpf = [t[:, :].bitcast(F32) for t in tp]

        x_in, w_in, b_in, const_set, const_done = (sem(n) for n in ("x_in", "w_in", "b_in", "const_set", "const_done"))
        grp_copied, grp_T, grp_Tcopied, grp_sup, grp_split, grp_step = (
            sem(n) for n in ("grp_copied", "grp_T", "grp_Tcopied", "grp_sup", "grp_split", "grp_step"))
        bias_added, w_zeroed, pads_zeroed = (sem(n) for n in ("bias_added", "w_zeroed", "pads_zeroed"))
        a_load = [sem(f"a_load{k}") for k in range(SLOTS)]
        tp_done, m_ready, ct_done, v_ready, w_ready, sup_done, acc_read = (
            sem(n) for n in ("tp_done", "m_ready", "ct_done", "v_ready", "w_ready", "sup_done", "acc_read"))
        ln_step, var_ready, sd_ready = (sem(n) for n in ("ln_step", "var_ready", "sd_ready"))
        xn_ready, xT_done, xT_copied = (sem(n) for n in ("xn_ready", "xT_done", "xT_copied"))
        xi_ready, g_ready, g_used, out_sent, y_free = (sem(n) for n in ("xi_ready", "g_ready", "g_used", "out_sent", "y_free"))
        y_ready = sem("y_ready")
        load_turn, product_turn = sem("load_turn"), sem("product_turn")

        block = ctx.enter_context(nc.Block())

        LN_STEPS = 13
        EPI_STEPS = 3 + LN_STEPS
        TP_CREDIT = STEPS
        MASK_CREDIT = 2
        WGT_CREDIT = 2 * CHAINS
        G_CREDIT = SLOTS * TI
        ONE = 1
        L0_LN = NS * EPI_STEPS
        L1_STEPS = 5 + LN_STEPS

        @block.sync
        def _(sp):
            sp.dma_start(x_all[:, :, :], x_v).then_inc(x_in, 16)
            sp.wait_ge(w_zeroed, 1)
            sp.dma_start(w_sb[0:D, :], weight).then_inc(w_in, 16)
            sp.dma_start(bias_sb[:, :], bias.partition_broadcast(P)).then_inc(b_in, 16)
            with sp.Fori(0, NS) as s:
                with sp.Fori(0, BODIES) as g:
                    down = sp.snap(BODIES - 1 - g)
                    for k in range(SLOTS):
                        j0 = down * (SLOTS * CJ) + (SLOTS - 1 - k) * CJ
                        sp.wait_ge(tp_done, (s * BODIES + g) * STEPS + (k + 1) * TJ)
                        sp.sem_inc(load_turn, 1)
                        sp.dma_start(A[k][:, :, :], adj_v[s, :, :, bass.ds(j0, CJ)]).then_inc(a_load[k], 16)
            sp.wait_ge(tp_done, TP_CREDIT + NS * NB)
            with sp.Fori(0, NS) as s:
                with sp.Fori(0, BODIES) as g:
                    down = sp.snap(BODIES - 1 - g)
                    for k in range(SLOTS):
                        j0 = down * (SLOTS * CJ) + (SLOTS - 1 - k) * CJ
                        sp.wait_ge(g_used, (s * BODIES + g) * SLOTS * TI + (k + 1) * TI)
                        sp.sem_inc(load_turn, 1)
                        sp.dma_start(A[k][:, :, :], adj_v[s, :, :, bass.ds(j0, CJ)]).then_inc(a_load[k], 16)
            sp.wait_ge(out_sent, 16 * (NS + 1))

        @block.gpsimd
        def _(pool):
            pool.memset(ident[:, :], 0.0).then_inc(const_set, 1)
            pool.memset(w_sb[:, :], 0.0).then_inc(w_zeroed, 1)
            pool.memset(x_group[:, :, :], 0.0).then_inc(pads_zeroed, 1)
            pool.memset(strip_pad[:, :, :], 0.0).then_inc(pads_zeroed, 1)
            pool.memset(zeros[:, :], 0.0).then_inc(const_set, 1)
            pool.memset(count_w[:, :], -1.0).then_inc(const_set, 1)
            pool.memset(carry_w[:, :], -1.0).then_inc(const_set, 1)
            pool.wait_ge(const_set, 4)
            pool.affine_select(out=ident[:, :], in_=ident[:, :], compare_op=ALU.not_equal, fill=1.0,
                               base=0, pattern=[[-1, P]], channel_multiplier=1).then_inc(const_set, 1)
            pool.affine_select(out=count_w[:, :], in_=count_w[:, :], compare_op=ALU.is_ge, fill=0.0,
                               base=0, pattern=[[-1, P]], channel_multiplier=1).then_inc(const_set, 1)
            pool.affine_select(out=carry_w[:, :], in_=carry_w[:, :], compare_op=ALU.is_ge, fill=0.0,
                               base=0, pattern=[[1, P]], channel_multiplier=-1).then_inc(const_set, 1)
            pool.wait_ge(const_set, 7)
            pool.tensor_copy(ident_b[:, :], ident[:, :]).then_inc(const_done, 1)
            pool.affine_select(out=count_w[:, :], in_=count_w[:, :], compare_op=ALU.not_equal, fill=float(MAX_NEIGH),
                               base=0, pattern=[[-1, P]], channel_multiplier=1).then_inc(const_done, 1)
            pool.affine_select(out=carry_w[:, :], in_=carry_w[:, :], compare_op=ALU.not_equal,
                               fill=float(-1 - MAX_NEIGH), base=0, pattern=[[-1, P]],
                               channel_multiplier=1).then_inc(const_done, 1)
            pool.wait_ge(b_in, 16)
            pool.wait_ge(grp_copied, NS + ONE)
            pool.tensor_tensor(x_all[:, :, :], x_all[:, :, :],
                               bias_sb[:, :].unsqueeze(1).to_broadcast([P, NB, D]), ALU.add).then_inc(bias_added, 1)

        def normalise(dve, strip_, dst, base, count0):
            def after(k):
                dve.wait_ge(ln_step, base + k)

            def cast(c):
                return c[:, :].unsqueeze(2).to_broadcast([P, TI, D])
            total, mean, total2, var, q, inv, sd, rec = col
            nc.vector.tensor_reduce(total[:, :], strip_, AXX, ALU.add).then_inc(ln_step, 1)
            after(1)
            nc.vector.tensor_scalar(mean[:, :], total[:, :], 1.0 / D, None, ALU.mult).then_inc(ln_step, 1)
            after(2)
            nc.vector.tensor_tensor(strip_, strip_, cast(mean), ALU.subtract).then_inc(ln_step, 1)
            after(3)
            nc.vector.tensor_tensor(square[:, :, :], strip_, strip_, ALU.mult).then_inc(ln_step, 1)
            after(4)
            nc.vector.tensor_reduce(total2[:, :], square[:, :, :], AXX, ALU.add).then_inc(ln_step, 1)
            after(5)
            nc.vector.tensor_scalar(var[:, :], total2[:, :], 1.0 / D, EPS, ALU.mult, ALU.add).then_inc(ln_step, 1)
            dve.wait_ge(sd_ready, count0 + 1)
            nc.vector.reciprocal(rec[:, :], sd[:, :]).then_inc(ln_step, 1)
            after(7)
            nc.vector.tensor_tensor(q[:, :], var[:, :], rec[:, :], ALU.mult).then_inc(ln_step, 1)
            after(8)
            nc.vector.tensor_tensor(q[:, :], q[:, :], sd[:, :], ALU.add).then_inc(ln_step, 1)
            after(9)
            nc.vector.tensor_scalar(q[:, :], q[:, :], 0.5, None, ALU.mult).then_inc(ln_step, 1)
            after(10)
            nc.vector.reciprocal(inv[:, :], q[:, :]).then_inc(ln_step, 1)
            after(11)
            nc.vector.tensor_tensor(strip_, strip_, cast(inv), ALU.mult).then_inc(ln_step, 1)
            after(12)
            nc.vector.tensor_scalar(dst, strip_, 1.0, None, ALU.mult).then_inc(ln_step, 1)
            after(13)

        @block.scalar
        def _(act):
            def root(done):
                act.wait_ge(ln_step, done)
                nc.scalar.activation(col[6][:, :], col[3][:, :], ACT.Sqrt).then_inc(sd_ready, 1)

            act.sem_inc(grp_copied, ONE)
            act.sem_inc(grp_Tcopied, ONE)
            act.wait_ge(x_in, 16)
            act.wait_ge(pads_zeroed, 2)
            with act.Fori(0, NS) as s:
                act.wait_ge(grp_T, s + ONE)
                nc.scalar.copy(x_group[:, :, 0:D], x_all[:, bass.ds(s * TI, TI), :]).then_inc(grp_copied, 1)
                act.wait_ge(grp_T, s + 1 + ONE)
                act.wait_ge(grp_sup, s + ONE)
                for k in range(2):
                    nc.scalar.copy(x_groupT[:, k * 512:(k + 1) * 512], tpf[k][:, :]).then_inc(grp_Tcopied, 1)
            with act.Fori(0, NS) as s:
                def weights(u, g):
                    for c in range(CHAINS):
                        n2 = (s * NB + g * STEPS + u) * CHAINS + c
                        act.wait_ge(v_ready, n2 + 1)
                        act.wait_ge(sup_done, n2 + 1)
                        nc.scalar.activation(wgt[c][u % 2][:, :].bitcast(I16), count[c][:, :], ACT.Relu,
                                             scale=BF16_EXPONENT_STEP).then_inc(w_ready, 1)
                with act.Fori(0, BODIES) as g:
                    for u in range(STEPS):
                        weights(u, g)
                root(s * EPI_STEPS + 3 + 6)
                act.wait_ge(xT_done, s + 1)
                for k in range(2):
                    nc.scalar.copy(xT[:, bass.ds(s * STRIP + k * 512, 512)], tpf[k][:, :]).then_inc(xT_copied, 1)
            act.wait_ge(xT_copied, 2 * NS)
            with act.Fori(0, NS) as s:
                act.wait_ge(g_ready, s * (NQ * TI) + ONE)
                nc.scalar.copy(x_groupT[:, :], xT[:, bass.ds(s * STRIP, STRIP)]).then_inc(xi_ready, 1)
                root(s * L1_STEPS + 5 + 6 + L0_LN)
                act.wait_ge(y_ready, s + 1)
                act.dma_start(out_v[s], square[:, :, :]).then_inc(out_sent, 16)

        @block.vector
        def _(dve):
            dve.sem_inc(m_ready, MASK_CREDIT)
            dve.sem_inc(g_used, G_CREDIT)
            dve.sem_inc(out_sent, 16)
            dve.sem_inc(grp_split, ONE)
            dve.sem_inc(acc_read, ONE)
            with dve.Fori(0, NS) as s:
                dve.wait_ge(grp_sup, s + 1 + ONE)
                sup = acc[:, 0, :].rearrange("p (t d) -> p t d", d=D)

                def piece(k):
                    return support[:, bass.ds((s * TI), TI), k * D:(k + 1) * D]
                nc.vector.tensor_scalar(rest[:, :, :], sup, WEIGHT_SHIFT, None, ALU.mult).then_inc(grp_split, 1)
                dve.wait_ge(grp_split, s + 1 + ONE)
                nc.vector.tensor_scalar(piece(0), rest[:, :, :], 1.0, None, ALU.mult).then_inc(grp_step, 1)
                dve.wait_ge(grp_step, s * 4 + 1)
                nc.vector.tensor_tensor(rest2[:, :, :], rest[:, :, :], piece(0), ALU.subtract).then_inc(grp_step, 1)
                dve.wait_ge(grp_step, s * 4 + 2)
                nc.vector.tensor_scalar(piece(1), rest2[:, :, :], 1.0, None, ALU.mult).then_inc(grp_step, 1)
                dve.wait_ge(grp_step, s * 4 + 3)
                nc.vector.tensor_tensor(piece(2), rest2[:, :, :], piece(1), ALU.subtract).then_inc(grp_step, 1)
            with dve.Fori(0, NS) as s:
                with dve.Fori(0, BODIES) as g:
                    for u in range(STEPS):
                        n = s * NB + g * STEPS + u
                        dve.wait_ge(tp_done, n + 1 + TP_CREDIT)
                        dve.wait_ge(ct_done, n + 1)
                        nc.vector.tensor_scalar(mask[u % 2][:, :], tp[u % 2][:, :], 0.0, None,
                                                ALU.not_equal).then_inc(m_ready, 1)
                dve.wait_ge(sup_done, (s + 1) * (NB * CHAINS) + WGT_CREDIT)
                dve.wait_ge(bias_added, 1)
                base = s * EPI_STEPS
                strip_v = strip.rearrange("p (b h) d -> p b h d", h=2)
                nc.vector.tensor_copy(strip_v, acc_v[:, :, :, 2 * D:3 * D]).then_inc(ln_step, 1)
                dve.wait_ge(ln_step, base + 1)
                nc.vector.tensor_tensor(strip_v, strip_v, acc_v[:, :, :, D:2 * D], ALU.add).then_inc(ln_step, 1)
                dve.wait_ge(ln_step, base + 2)
                nc.vector.tensor_tensor(strip_v, strip_v, acc_v[:, :, :, 0:D], ALU.add).then_inc(acc_read, 1)
                dve.wait_ge(acc_read, s + 1 + ONE)
                rows = x_all[:, bass.ds(s * TI, TI), :]
                nc.vector.tensor_tensor(strip, strip, rows, ALU.add).then_inc(ln_step, 1)
                dve.wait_ge(ln_step, base + 3)
                normalise(dve, strip, rows, base + 3, s)
                dve.wait_ge(xT_done, s + 1)
            with dve.Fori(0, NS) as s:
                with dve.Fori(0, BODIES) as g:
                    for k in range(SLOTS):
                        dve.wait_ge(a_load[k], ((s + NS) * BODIES + g + 1) * 16)
                        for t in range(TI):
                            n = ((s * BODIES + g) * SLOTS + k) * TI + t
                            dve.wait_ge(g_used, n - 1 + G_CREDIT)
                            dve.wait_ge(g_ready, n + 1 + ONE)
                            op = nc.vector.scalar_tensor_tensor(
                                junk[t % 2][:, :], acc[:, t % GRING, :], 1.0, A[k][:, t, :], ALU.mult, ALU.mult,
                                accum_out=part[:, t, bass.ds(g * SLOTS + k, 1)])
                            op.then_inc(g_used, 1)
                base = s * L1_STEPS + L0_LN
                dve.wait_ge(g_used, (s + 1) * NQ * TI + G_CREDIT)
                outer = col[0]
                rows = x_all[:, bass.ds(s * TI, TI), :]
                nc.vector.tensor_reduce(outer[:, :], part[:, :, :], AXX, ALU.add).then_inc(ln_step, 1)
                dve.wait_ge(ln_step, base + 1)
                nc.vector.tensor_scalar(outer[:, :], outer[:, :], R_CONST, None, ALU.mult).then_inc(ln_step, 1)
                nc.vector.tensor_scalar(strip, rows, -B_CONST, F_CONST, ALU.mult,
                                        ALU.add).then_inc(ln_step, 1)
                dve.wait_ge(ln_step, base + 3)
                nc.vector.tensor_tensor(strip, strip,
                                        outer[:, :].unsqueeze(2).to_broadcast([P, TI, D]),
                                        ALU.subtract).then_inc(ln_step, 1)
                dve.wait_ge(ln_step, base + 4)
                nc.vector.tensor_tensor(strip, strip, rows, ALU.add).then_inc(ln_step, 1)
                dve.wait_ge(ln_step, base + 5)
                dve.wait_ge(out_sent, (s + 1) * 16)
                normalise(dve, strip, square[:, :, :], base + 5, s + NS)
                dve.sem_inc(y_ready, 1)

        @block.tensor
        def _(pe):
            pe.sem_inc(ct_done, MASK_CREDIT)
            pe.sem_inc(tp_done, TP_CREDIT)
            pe.sem_inc(grp_T, ONE)
            pe.sem_inc(grp_sup, ONE)
            pe.sem_inc(g_ready, ONE)
            pe.sem_inc(sup_done, WGT_CREDIT)
            pe.wait_ge(w_in, 16)
            pe.wait_ge(const_done, 3)
            with pe.Fori(0, NS) as s:
                pe.wait_ge(grp_copied, s + 1 + ONE)
                pe.wait_ge(grp_Tcopied, 2 * s + ONE)
                for t in range(TI):
                    last = nc.tensor.transpose(tpf[t // 4][:, (t % 4) * P:(t % 4 + 1) * P], x_group[:, t, :],
                                               ident[:, :])
                last.then_inc(grp_T, 1)
                pe.wait_ge(grp_Tcopied, 2 * s + 2 + ONE)
                pe.wait_ge(grp_split, s + ONE)
                for t in range(TI):
                    last = nc.tensor.matmul(acc[:, 0, t * D:(t + 1) * D], x_groupT[:, t * P:(t + 1) * P], w_sb[:, :],
                                            start=True, stop=True)
                last.then_inc(grp_sup, 1)
            pe.wait_ge(grp_step, 4 * NS)
            pe.wait_ge(grp_split, NS + ONE)

            with pe.Fori(0, NS) as s:
                def transposes(u, g):
                    k, tj = u // TJ, TJ - 1 - u % TJ
                    n = s * NB + g * STEPS + u
                    if u % TJ == 0:
                        pe.wait_ge(a_load[k], (s * BODIES + g + 1) * 16)
                    pe.wait_ge(m_ready, n + 1)
                    for t in range(TI):
                        last = nc.tensor.transpose(tp[u % 2][:, t * P:(t + 1) * P],
                                                   A_high[k][:, t, 2 * tj * P + 1:2 * (tj + 1) * P:2], ident_b[:, :])
                    last.then_inc(tp_done, 1)

                def add_support(u, down, c):
                    jb = down * STEPS + (STEPS - 1 - u)
                    for t in range(TH):
                        i = c * TH + t
                        last = nc.tensor.matmul(acc[:, i // 2, (i % 2) * PIECES:(i % 2 + 1) * PIECES],
                                                wgt[c][u % 2][:, t * P:(t + 1) * P], support[:, jb, :],
                                                start=False, stop=True, skip_group_check=True)
                    last.then_inc(sup_done, 1)

                def step(u, g, down, first, last):
                    n = s * NB + g * STEPS + u
                    n2 = n * CHAINS
                    pe.wait_ge(m_ready, n + 1 + MASK_CREDIT)
                    for c in range(CHAINS):
                        nc.tensor.matmul(count[c][:, :], count_w[:, :], mask[u % 2][:, c * HALF:(c + 1) * HALF],
                                         start=False, stop=True, skip_group_check=True).then_inc(v_ready, 1)
                    if not first:
                        add_support((u - 1) % STEPS, down if u else down + 1, 1)
                    if not last:
                        transposes((u + 1) % STEPS, g if u + 1 < STEPS else g + 1)
                    for c in range(CHAINS):
                        pe.wait_ge(w_ready, n2 + c + 1)
                        m = nc.tensor.matmul(count[c][:, :], carry_w[:, :], mask[u % 2][:, c * HALF:(c + 1) * HALF],
                                             start=False, stop=True, skip_group_check=True)
                        if c == CHAINS - 1:
                            m.then_inc(ct_done, 1)
                        else:
                            add_support(u, down, c)
                    if last:
                        add_support(u, down, CHAINS - 1)

                for c in range(CHAINS):
                    nc.tensor.matmul(count[c][:, :], zeros[:, 0:P], zeros[:, 0:HALF], start=True, stop=True)
                pe.wait_ge(acc_read, s + ONE)
                for b in range(GRING):
                    nc.tensor.matmul(acc[:, b, 0:2 * PIECES], zeros[:, 0:P], zeros[:, 0:2 * PIECES],
                                     start=True, stop=True)
                transposes(0, 0)
                for u in range(STEPS):
                    step(u, 0, BODIES - 1, u == 0, False)
                with pe.Fori(1, BODIES - 1) as g:
                    down = pe.snap(BODIES - 1 - g)
                    for u in range(STEPS):
                        step(u, g, down, False, False)
                for u in range(STEPS):
                    step(u, BODIES - 1, 0, False, u == STEPS - 1)
                pe.wait_ge(ln_step, (s + 1) * EPI_STEPS)
                pe.wait_ge(m_ready, (s + 1) * NB + MASK_CREDIT)
                for t in range(TI):
                    last = nc.tensor.transpose(tpf[t // 4][:, (t % 4) * P:(t % 4 + 1) * P], strip_pad[:, t, :],
                                               ident[:, :])
                last.then_inc(xT_done, 1)
                pe.wait_ge(xT_copied, 2 * (s + 1))
            with pe.Fori(0, NS) as s:
                pe.wait_ge(xi_ready, s + 1)
                pe.sem_inc(product_turn, 1)
                with pe.Fori(0, BODIES) as g:
                    down = pe.snap(BODIES - 1 - g)
                    for k in range(SLOTS):
                        j0 = down * (SLOTS * CJ) + (SLOTS - 1 - k) * CJ
                        for t in range(TI):
                            n = ((s * BODIES + g) * SLOTS + k) * TI + t
                            pe.wait_ge(g_used, n + 1 + G_CREDIT - GRING)
                            pe.sem_inc(product_turn, 1)
                            nc.tensor.matmul(acc[:, t % GRING, :], x_groupT[:, t * P:(t + 1) * P],
                                             xT[:, bass.ds(j0, CJ)], start=True, stop=True).then_inc(g_ready, 1)


_INS = ['x', 'adj', 'L0_gnn_weight', 'L0_gnn_bias']
_OUTS = [((8192, 64), 'float32')]


def kernel(**inputs):
    import numpy as _np
    import concourse.bacc as _bacc
    from concourse import mybir as _mybir
    from concourse.bass_utils import run_bass_kernel_spmd as _run

    nc = _bacc.Bacc("TRN2", target_bir_lowering=False, num_devices=1)
    arrays, args = {}, []
    for name in _INS:
        a = _np.ascontiguousarray(inputs[name])
        arrays[f"in_{name}_dram"] = a
        args.append(nc.dram_tensor(f"in_{name}_dram", a.shape, _mybir.dt.from_np(a.dtype), kind="ExternalInput").ap())
    for i, (shape, dtype) in enumerate(_OUTS):
        dt = _mybir.dt.from_np(_np.dtype(dtype))
        args.append(nc.dram_tensor(f"out_{i}_dram", shape, dt, kind="ExternalOutput").ap())
    adj_resnorm_kernel(nc, *args)
    r = _run(nc, [arrays], core_ids=[0])
    got = tuple(r.results[0][f"out_{i}_dram"] for i in range(len(_OUTS)))
    return got[0]
```

```python
from contextlib import ExitStack

import concourse.bass as bass
from concourse import mybir

ALU = mybir.AluOpType
ACT = mybir.ActivationFunctionType
AXX = mybir.AxisListType.X
F32 = mybir.dt.float32
BF16 = mybir.dt.bfloat16
I16 = mybir.dt.int16
U16 = mybir.dt.uint16
I32 = mybir.dt.int32

P = 128
MAX_NEIGH = 100
EPS = 1e-5
F_CONST, B_CONST, R_CONST = 1.0, 0.1, 0.01
WEIGHT_SHIFT = 2.0 ** (127 - MAX_NEIGH)
BF16_EXPONENT_STEP = 128.0


def adj_resnorm_kernel(nc, x, adj, weight, bias, out):
    N, D = x.shape
    NB = N // P
    TI = 8
    STRIP = TI * P
    NS = N // STRIP
    CJ = 512
    NQ = N // CJ
    TJ = CJ // P
    SLOTS = 4
    STEPS = SLOTS * TJ
    BODIES = NB // STEPS
    GROUPS = NS * BODIES
    CHAINS = 2
    HALF = STRIP // CHAINS
    TH = HALF // P
    PIECES = 3 * D
    GRING = 4
    ONE_BIT = 14
    MASK_ONE = 2.0

    adj_v = adj.rearrange("(s t p) j -> s p t j", t=TI, p=P)
    x_v = x.rearrange("(b p) d -> p b d", p=P)
    out_v = out.rearrange("(s t p) d -> s p t d", t=TI, p=P)

    ctx = ExitStack()
    with ctx:
        def sb(name, shape, dt):
            return ctx.enter_context(nc.sbuf_tensor(name, shape, dt))

        def pb(name, shape, dt):
            return ctx.enter_context(nc.psum_tensor(name, shape, dt))

        def sem(name):
            return ctx.enter_context(nc.semaphore(name))

        A = [sb(f"A{k}", [P, TI, CJ], F32) for k in range(SLOTS)]
        A_high = [a[:, :, :].bitcast(BF16) for a in A]
        bits = sb("bits", [P, GROUPS, STRIP], U16)
        x_all = sb("x_all", [P, NB, D], F32)
        w_sb = sb("w_sb", [P, D], F32)
        bias_sb = sb("bias_sb", [P, D], F32)
        support = sb("support", [P, NB, PIECES], BF16)
        y = sb("y", [P, TI, D], F32)
        square = sb("square", [P, TI, D], F32)
        rest, rest2 = y, square
        x_group = sb("x_group", [P, TI, P], F32)
        x_groupT = sb("x_groupT", [P, STRIP], F32)
        ident = sb("ident", [P, P], F32)
        ident_b = sb("ident_b", [P, P], BF16)
        bit_ident = sb("bit_ident", [P, STEPS, P], BF16)
        count_w = sb("count_w", [P, P], BF16)
        carry_w = sb("carry_w", [P, P], BF16)
        zeros = sb("zeros", [P, 512], BF16)
        ones = sb("ones", [P, 1], F32)
        mask = [sb(f"mask{k}", [P, STRIP], BF16) for k in range(2)]
        wgt = [[sb(f"wgt{c}{k}", [P, HALF], BF16) for k in range(2)] for c in range(CHAINS)]
        strip_pad = sb("strip_pad", [P, TI, P], F32)
        strip = strip_pad[:, :, 0:D]
        junk = [sb(f"junk{k}", [P, STRIP], BF16) for k in range(2)]
        odd = sb("odd", [P, GROUPS * STEPS], F32)
        odd_sum = sb("odd_sum", [P, 1], F32)
        flag = sb("flag", [1, 1], I32)
        minus_half = sb("minus_half", [P, TI], F32)
        col = [sb(f"col{k}", [P, TI], F32) for k in range(4)]

        xT = bits[:, 0:2 * NS, :].rearrange("p g i -> p (g i)").bitcast(F32)
        part = bits[:, 2 * NS, 0:2 * TI * NQ].bitcast(F32).rearrange("p (t q) -> p t q", q=NQ)

        banks = pb("banks", [P, 2 * GRING, 512], F32)
        sums = [banks[:, k * GRING:(k + 1) * GRING, :] for k in range(2)]
        sums_v = [a[:, :, 0:2 * PIECES].rearrange("p b (h c) -> p b h c", h=2) for a in sums]
        acc, acc_v = sums[0], sums_v[0]
        count = [banks[:, GRING + c, :] for c in range(CHAINS)]
        word_half = [banks[:, GRING + CHAINS + k, :] for k in range(2)]
        word = banks[:, GRING + CHAINS:GRING + CHAINS + 2, :].rearrange("p b i -> p (b i)")
        tp = [w.bitcast(BF16) for w in word_half]
        strip_h = strip.rearrange("p (b h) d -> p b h d", h=2)

        x_in, w_in, b_in, const_set, const_done = (sem(n) for n in ("x_in", "w_in", "b_in", "const_set", "const_done"))
        grp_copied, grp_T, grp_Tcopied, grp_sup, grp_split, grp_step = (
            sem(n) for n in ("grp_copied", "grp_T", "grp_Tcopied", "grp_sup", "grp_split", "grp_step"))
        bias_added, w_zeroed, pads_zeroed = (sem(n) for n in ("bias_added", "w_zeroed", "pads_zeroed"))
        load_turn = sem("load_turn")
        product_turn = sem("product_turn")
        a_load = [sem(f"a_load{k}") for k in range(SLOTS)]
        tile_done, tile_tested, word_read = (sem(n) for n in ("tile_done", "tile_tested", "word_read"))
        m_ready, ct_done, v_ready, w_ready, sup_done, acc_read = (
            sem(n) for n in ("m_ready", "ct_done", "v_ready", "w_ready", "sup_done", "acc_read"))
        ln_step, var_ready, root_ready = (sem(n) for n in ("ln_step", "var_ready", "root_ready"))
        odd_ready, odd_total, flag_ready = (sem(n) for n in ("odd_ready", "odd_total", "flag_ready"))
        m1_ready, m1_used, pieces_step, pieces_ready, ln1_step = (
            sem(n) for n in ("m1_ready", "m1_used", "pieces_step", "pieces_ready", "ln1_step"))
        support_ready, pieces_split = sem("support_ready"), sem("pieces_split")
        y_ready, out_sent = sem("y_ready"), sem("out_sent")
        g_load = [sem(f"g_load{k}") for k in range(SLOTS)]
        (g_x_in, g_bias_added, g_tp_done, g_m_ready, g_ct_done, g_v_ready, g_w_ready, g_sup_done, g_acc_read,
         g_ln_step, g_var_ready, g_root_ready, g_xT_done, g_xT_copied, g_xi_ready, g_ready, g_used, g_y_ready,
         g_out_sent) = (sem("g_" + n) for n in (
             "x_in", "bias_added", "tp_done", "m_ready", "ct_done", "v_ready", "w_ready", "sup_done", "acc_read",
             "ln_step", "var_ready", "root_ready", "xT_done", "xT_copied", "xi_ready", "ready", "used", "y_ready",
             "out_sent"))

        block = ctx.enter_context(nc.Block())

        LOAD_CREDIT = STEPS
        MASK_CREDIT = 2
        WGT_CREDIT = 2 * CHAINS
        G_CREDIT = SLOTS * TI
        ONE = 1

        SUMS, NORM = 3, 7
        L0_END = (SUMS - 1) + 1 + (NORM - 1)
        L1_END = (SUMS - 1) + 2 + 4 + (NORM - 1)
        G0_END, G1_END = L0_END + 1, 1 + 4 + (NORM - 1)
        FINISH0, FINISH1 = SUMS + 1 + NORM, SUMS + 2 + 4 + NORM
        WORDS_AT = 13
        TILES_AT = [[u] for u in range(10)] + [[10, 11], [12, 13], [14, 15], [], [], []]

        def across(c):
            return c[:, :].unsqueeze(2).to_broadcast([P, TI, D])

        @block.sync
        def _(sp):
            sp.dma_start(x_all[:, :, :], x_v).then_inc(x_in, 16)
            sp.wait_ge(w_zeroed, 1)
            sp.dma_start(w_sb[0:D, :], weight).then_inc(w_in, 16)
            sp.dma_start(bias_sb[:, :], bias.partition_broadcast(P)).then_inc(b_in, 16)
            with sp.Fori(0, NS) as s:
                with sp.Fori(0, BODIES) as g:
                    down = sp.snap(BODIES - 1 - g)
                    for k in range(SLOTS):
                        j0 = down * (SLOTS * CJ) + (SLOTS - 1 - k) * CJ
                        used = (s * BODIES + g) * STEPS + (k + 1) * TJ
                        sp.wait_ge(tile_tested, used)
                        sp.wait_ge(tile_done, used)
                        sp.sem_inc(load_turn, 1)
                        sp.dma_start(A[k][:, :, :], adj_v[s, :, :, bass.ds(j0, CJ)]).then_inc(a_load[k], 16)
            sp.wait_ge(flag_ready, 1)
            general = sp.value_load(flag[0:1, 0:1])
            with sp.If(general != 0):
                sp.dma_start(x_all[:, :, :], x_v).then_inc(g_x_in, 16)
                with sp.Fori(0, NS) as s:
                    with sp.Fori(0, BODIES) as g:
                        down = sp.snap(BODIES - 1 - g)
                        for k in range(SLOTS):
                            j0 = down * (SLOTS * CJ) + (SLOTS - 1 - k) * CJ
                            sp.wait_ge(g_tp_done, (s * BODIES + g) * STEPS + (k + 1) * TJ)
                            sp.sem_inc(load_turn, 1)
                            sp.dma_start(A[k][:, :, :], adj_v[s, :, :, bass.ds(j0, CJ)]).then_inc(g_load[k], 16)
                sp.wait_ge(g_tp_done, LOAD_CREDIT + NS * NB)
                with sp.Fori(0, NS) as s:
                    with sp.Fori(0, BODIES) as g:
                        down = sp.snap(BODIES - 1 - g)
                        for k in range(SLOTS):
                            j0 = down * (SLOTS * CJ) + (SLOTS - 1 - k) * CJ
                            sp.wait_ge(g_used, (s * BODIES + g) * SLOTS * TI + (k + 1) * TI)
                            sp.sem_inc(load_turn, 1)
                            sp.dma_start(A[k][:, :, :], adj_v[s, :, :, bass.ds(j0, CJ)]).then_inc(g_load[k], 16)
                sp.wait_ge(g_out_sent, 16 * (NS + 1))
            with sp.Else():
                with sp.Fori(0, NS) as s:
                    sp.wait_ge(y_ready, s + 1)
                    sp.sem_inc(load_turn, 1)
                    sp.dma_start(out_v[s], y[:, :, :]).then_inc(out_sent, 16)
                sp.wait_ge(out_sent, 16 * (NS + 1))
            sp.nop()

        @block.gpsimd
        def _(pool):
            pool.memset(w_sb[:, :], 0.0).then_inc(w_zeroed, 1)
            pool.memset(x_group[:, :, :], 0.0).then_inc(pads_zeroed, 1)
            pool.memset(strip_pad[:, :, :], 0.0).then_inc(pads_zeroed, 1)
            pool.memset(zeros[:, :], 0.0).then_inc(const_set, 1)
            pool.memset(ones[:, :], 1.0).then_inc(const_set, 1)
            pool.memset(minus_half[:, :], -0.5).then_inc(const_set, 1)
            pool.memset(ident[:, :], 0.0).then_inc(const_set, 1)
            pool.memset(count_w[:, :], -1.0 / MASK_ONE).then_inc(const_set, 1)
            pool.memset(carry_w[:, :], -1.0 / MASK_ONE).then_inc(const_set, 1)
            pool.wait_ge(const_set, 6)
            pool.affine_select(out=ident[:, :], in_=ident[:, :], compare_op=ALU.not_equal, fill=1.0,
                               base=0, pattern=[[-1, P]], channel_multiplier=1).then_inc(const_set, 1)
            pool.affine_select(out=count_w[:, :], in_=count_w[:, :], compare_op=ALU.is_ge, fill=0.0,
                               base=0, pattern=[[-1, P]], channel_multiplier=1).then_inc(const_set, 1)
            pool.affine_select(out=carry_w[:, :], in_=carry_w[:, :], compare_op=ALU.is_ge, fill=0.0,
                               base=0, pattern=[[1, P]], channel_multiplier=-1).then_inc(const_set, 1)
            pool.wait_ge(const_set, 9)
            for v in range(STEPS):
                pool.tensor_scalar(bit_ident[:, v, :], ident[:, :], float(1 << v), None,
                                   ALU.mult).then_inc(const_done, 1)
            pool.tensor_copy(ident_b[:, :], ident[:, :]).then_inc(const_done, 1)
            pool.affine_select(out=count_w[:, :], in_=count_w[:, :], compare_op=ALU.not_equal,
                               fill=MAX_NEIGH / MASK_ONE, base=0, pattern=[[-1, P]],
                               channel_multiplier=1).then_inc(const_done, 1)
            pool.affine_select(out=carry_w[:, :], in_=carry_w[:, :], compare_op=ALU.not_equal,
                               fill=(-1 - MAX_NEIGH) / MASK_ONE, base=0, pattern=[[-1, P]],
                               channel_multiplier=1).then_inc(const_done, 1)
            pool.wait_ge(b_in, 16)
            pool.wait_ge(grp_copied, NS + ONE)
            pool.tensor_tensor(x_all[:, :, :], x_all[:, :, :],
                               bias_sb[:, :].unsqueeze(1).to_broadcast([P, NB, D]), ALU.add).then_inc(bias_added, 1)

            def root(ready, n, done):
                pool.wait_ge(ready, n + 1)
                pool.tensor_tensor(col[3][:, :], col[2][:, :], minus_half[:, :], ALU.pow).then_inc(done, 1)

            with pool.Fori(0, NS) as s:
                root(var_ready, s, root_ready)
            pool.wait_ge(flag_ready, 1)
            general = pool.value_load(flag[0:1, 0:1])
            with pool.If(general != 0):
                pool.wait_ge(g_x_in, 16)
                pool.tensor_tensor(x_all[:, :, :], x_all[:, :, :], bias_sb[:, :].unsqueeze(1).to_broadcast([P, NB, D]),
                                   ALU.add).then_inc(g_bias_added, 1)
                with pool.Fori(0, 2 * NS) as s:
                    root(g_var_ready, s, g_root_ready)
            with pool.Else():
                with pool.Fori(NS, 2 * NS) as s:
                    root(var_ready, s, root_ready)
            pool.nop()

        @block.scalar
        def _(act):
            act.sem_inc(grp_copied, ONE)
            act.sem_inc(grp_Tcopied, ONE)
            act.wait_ge(x_in, 16)
            act.wait_ge(pads_zeroed, 2)
            with act.Fori(0, NS) as s:
                act.wait_ge(grp_T, s + ONE)
                nc.scalar.copy(x_group[:, :, 0:D], x_all[:, bass.ds(s * TI, TI), :]).then_inc(grp_copied, 1)
                act.wait_ge(grp_T, s + 1 + ONE)
                act.wait_ge(grp_sup, s + ONE)
                for k in range(2):
                    nc.scalar.copy(x_groupT[:, k * 512:(k + 1) * 512], word_half[k]).then_inc(grp_Tcopied, 1)

            def weights(u, n, counted, used, ready):
                for c in range(CHAINS):
                    act.wait_ge(counted, n * CHAINS + c + 1)
                    act.wait_ge(used, n * CHAINS + c + 1)
                    nc.scalar.activation(wgt[c][u % 2][:, :].bitcast(I16), count[c][:, :], ACT.Relu,
                                         scale=BF16_EXPONENT_STEP).then_inc(ready, 1)

            with act.Fori(0, GROUPS) as g:
                for u in range(STEPS):
                    weights(u, g * STEPS + u, v_ready, sup_done, w_ready)
            act.wait_ge(flag_ready, 1)
            general = act.value_load(flag[0:1, 0:1])
            with act.If(general != 0):
                with act.Fori(0, NS) as s:
                    with act.Fori(0, BODIES) as g:
                        for u in range(STEPS):
                            weights(u, (s * BODIES + g) * STEPS + u, g_v_ready, g_sup_done, g_w_ready)
                    act.wait_ge(g_xT_done, s + 1)
                    for k in range(2):
                        nc.scalar.copy(xT[:, bass.ds(s * STRIP + k * 512, 512)],
                                       word_half[k]).then_inc(g_xT_copied, 1)
                act.wait_ge(g_xT_copied, 2 * NS)
                with act.Fori(0, NS) as s:
                    act.wait_ge(g_ready, s * (NQ * TI) + ONE)
                    nc.scalar.copy(x_groupT[:, :], xT[:, bass.ds(s * STRIP, STRIP)]).then_inc(g_xi_ready, 1)
                    act.wait_ge(g_y_ready, s + 1)
                    act.dma_start(out_v[s], y[:, :, :]).then_inc(g_out_sent, 16)
            act.nop()

        @block.vector
        def _(dve):
            dve.sem_inc(grp_split, ONE)
            dve.sem_inc(acc_read, ONE)
            dve.sem_inc(word_read, ONE)
            dve.sem_inc(tile_tested, LOAD_CREDIT)
            for step in (grp_step, support_ready, ln_step, ln1_step, pieces_step, pieces_split, pieces_ready):
                dve.sem_inc(step, ONE)
            dve.sem_inc(out_sent, 16)

            def after(step, n):
                dve.wait_ge(step, n + ONE)

            def split(src, factor, blocks, step, turn, copied):
                def part_of(k):
                    return support[:, blocks, k * D:(k + 1) * D]
                nc.vector.tensor_scalar(rest[:, :, :], src, factor, None, ALU.mult).then_inc(copied, 1)
                after(copied, turn + 1)
                nc.vector.tensor_scalar(part_of(0), rest[:, :, :], 1.0, None, ALU.mult).then_inc(step, 1)
                after(step, turn * 3 + 1)
                nc.vector.tensor_tensor(rest2[:, :, :], rest[:, :, :], part_of(0), ALU.subtract).then_inc(step, 1)
                after(step, turn * 3 + 2)
                nc.vector.tensor_scalar(part_of(1), rest2[:, :, :], 1.0, None, ALU.mult).then_inc(step, 1)
                after(step, turn * 3 + 3)
                return nc.vector.tensor_tensor(part_of(2), rest2[:, :, :], part_of(1), ALU.subtract)

            with dve.Fori(0, NS) as s:
                dve.wait_ge(grp_sup, s + 1 + ONE)
                split(acc[:, 0, :].rearrange("p (t d) -> p t d", d=D), WEIGHT_SHIFT, bass.ds(s * TI, TI), grp_step,
                      s, grp_split).then_inc(support_ready, 1)
                after(support_ready, s + 1)

            def sum_parts(k, acc_v, step, base, read, turn):
                after(step, base + k)
                if k == 0:
                    nc.vector.tensor_scalar(strip_h, acc_v[:, :, :, 2 * D:3 * D], 1.0, None, ALU.mult).then_inc(step, 1)
                elif k == 1:
                    nc.vector.tensor_tensor(strip_h, strip_h, acc_v[:, :, :, D:2 * D], ALU.add).then_inc(step, 1)
                else:
                    nc.vector.tensor_tensor(strip_h, strip_h, acc_v[:, :, :, 0:D], ALU.add).then_inc(read, 1)
                    after(read, turn + 1)

            def normalise(k, step, base, n, ready, done, dst):
                total, mean, var, inv = col
                if k != NORM - 1:
                    after(step, base + k)
                if k == 0:
                    nc.vector.tensor_reduce(total[:, :], strip, AXX, ALU.add).then_inc(step, 1)
                elif k == 1:
                    nc.vector.tensor_scalar(mean[:, :], total[:, :], 1.0 / D, None, ALU.mult).then_inc(step, 1)
                elif k == 2:
                    nc.vector.tensor_tensor(strip, strip, across(mean), ALU.subtract).then_inc(step, 1)
                elif k == 3:
                    nc.vector.tensor_tensor(square[:, :, :], strip, strip, ALU.mult).then_inc(step, 1)
                elif k == 4:
                    nc.vector.tensor_reduce(total[:, :], square[:, :, :], AXX, ALU.add).then_inc(step, 1)
                elif k == 5:
                    nc.vector.tensor_scalar(var[:, :], total[:, :], 1.0 / D, EPS, ALU.mult, ALU.add).then_inc(ready, 1)
                else:
                    dve.wait_ge(done, n + 1)
                    nc.vector.tensor_tensor(dst, strip, across(inv), ALU.mult).then_inc(step, 1)

            def combine(k, step, base, rows):
                outer = col[0]
                if k != 1:
                    after(step, base + k)
                if k == 0:
                    nc.vector.tensor_scalar(outer[:, :], outer[:, :], R_CONST, None, ALU.mult).then_inc(step, 1)
                elif k == 1:
                    nc.vector.tensor_scalar(strip, rows, -B_CONST, F_CONST, ALU.mult, ALU.add).then_inc(step, 1)
                elif k == 2:
                    nc.vector.tensor_tensor(strip, strip, across(outer), ALU.subtract).then_inc(step, 1)
                else:
                    nc.vector.tensor_tensor(strip, strip, rows, ALU.add).then_inc(step, 1)

            def rows_of(s):
                return x_all[:, bass.ds(s * TI, TI), :]

            def finish0(k, s):
                base = s * L0_END
                if k == 0:
                    dve.wait_ge(sup_done, (s + 1) * (NB * CHAINS) + WGT_CREDIT)
                    dve.wait_ge(bias_added, 1)
                if k < SUMS:
                    sum_parts(k, acc_v, ln_step, base, acc_read, s)
                elif k == SUMS:
                    nc.vector.tensor_tensor(strip, strip, rows_of(s), ALU.add).then_inc(ln_step, 1)
                else:
                    normalise(k - SUMS - 1, ln_step, base + SUMS, s, var_ready, root_ready, rows_of(s))

            def finish1(k, s, half):
                base = s * L1_END
                if k == 0:
                    dve.wait_ge(m1_used, (s + 1) * NB + MASK_CREDIT)
                if k < SUMS:
                    sum_parts(k, sums_v[half], ln1_step, base, acc_read, s + NS)
                elif k == SUMS:
                    nc.vector.tensor_tensor(square[:, :, :], strip, rows_of(s), ALU.mult).then_inc(ln1_step, 1)
                elif k == SUMS + 1:
                    after(ln1_step, base + SUMS)
                    nc.vector.tensor_reduce(col[0][:, :], square[:, :, :], AXX, ALU.add).then_inc(ln1_step, 1)
                elif k < SUMS + 6:
                    combine(k - SUMS - 2, ln1_step, base + SUMS + 1, rows_of(s))
                else:
                    if k == FINISH1 - 1:
                        dve.wait_ge(out_sent, (s + 1) * 16)
                    normalise(k - SUMS - 6, ln1_step, base + SUMS + 5, s + NS, var_ready, root_ready, y[:, :, :])
                    if k == FINISH1 - 1:
                        after(ln1_step, base + L1_END)
                        dve.sem_inc(y_ready, 1)

            def unpack(u, word16, dst, ready):
                if u <= ONE_BIT:
                    ops = (ONE_BIT - u, 1 << ONE_BIT, ALU.logical_shift_left, ALU.bitwise_and)
                else:
                    ops = (u - ONE_BIT, 1 << ONE_BIT, ALU.logical_shift_right, ALU.bitwise_and)
                nc.vector.tensor_scalar(dst[:, :].bitcast(U16), word16, *ops).then_inc(ready, 1)

            def next_mask(u, g):
                dve.wait_ge(ct_done, g * STEPS + u + 1)
                unpack(u, bits[:, bass.ds(g, 1), :].rearrange("p g i -> p (g i)"), mask[u % 2], m_ready)

            def read_words(g):
                dve.wait_ge(tile_done, (g + 1) * STEPS + LOAD_CREDIT)
                nc.vector.tensor_scalar(bits[:, bass.ds(g, 1), :].rearrange("p g i -> p (g i)"), word[:, :], 1.0, None,
                                        ALU.mult).then_inc(word_read, 1)
                dve.wait_ge(word_read, g + 1 + ONE)

            def test(u, g):
                k, tj = u // TJ, TJ - 1 - u % TJ
                if u % TJ == 0:
                    dve.wait_ge(a_load[k], (g + 1) * 16)
                tile = A[k][:, :, tj * P:(tj + 1) * P]
                dve.wait_ge(tile_tested, g * STEPS + u - 1 + LOAD_CREDIT)
                nc.vector.scalar_tensor_tensor(junk[u % 2][:, :].rearrange("p (t j) -> p t j", t=TI), tile, 1.0, tile,
                                               ALU.is_equal, ALU.not_equal,
                                               accum_out=odd[:, bass.ds(g * STEPS + u, 1)]).then_inc(tile_tested, 1)

            def body0(s, g, finish, last=False):
                n = s * BODIES + g
                for u in range(STEPS):
                    if finish and u == 0:
                        for k in range(SUMS):
                            finish0(k, s - 1)
                    elif finish and u + SUMS - 1 < FINISH0:
                        finish0(u + SUMS - 1, s - 1)
                    if u + 1 < STEPS:
                        next_mask(u + 1, n)
                    if not last:
                        if u == WORDS_AT:
                            read_words(n + 1)
                        test(u, n + 1)
                if not last:
                    next_mask(0, n + 1)

            for u in range(STEPS):
                test(u, 0)
            read_words(0)
            next_mask(0, 0)
            with dve.Fori(0, BODIES) as g:
                body0(0, g, False)
            with dve.Fori(1, NS - 1) as s:
                body0(s, 0, True)
                with dve.Fori(1, BODIES) as g:
                    body0(s, g, False)
            body0(NS - 1, 0, True)
            with dve.Fori(1, BODIES - 1) as g:
                body0(NS - 1, g, False)
            body0(NS - 1, BODIES - 1, False, True)
            for k in range(FINISH0):
                finish0(k, NS - 1)

            dve.wait_ge(tile_tested, NS * NB + LOAD_CREDIT)
            nc.vector.tensor_reduce(odd_sum[:, :], odd[:, :], AXX, ALU.add).then_inc(odd_ready, 1)
            dve.wait_ge(odd_total, 1)
            nc.vector.tensor_copy(flag[:, :], count[0][0:1, 0:1]).then_inc(flag_ready, 1)
            dve.wait_ge(flag_ready, 1)
            after(ln_step, NS * L0_END)
            general = dve.value_load(flag[0:1, 0:1])
            with dve.If(general != 0):
                dve.sem_inc(g_m_ready, MASK_CREDIT)
                dve.sem_inc(g_used, G_CREDIT)
                dve.sem_inc(g_out_sent, 16)
                dve.sem_inc(g_acc_read, ONE)
                dve.sem_inc(g_ln_step, ONE)
                with dve.Fori(0, NS) as s:
                    with dve.Fori(0, BODIES) as g:
                        for u in range(STEPS):
                            n = s * NB + g * STEPS + u
                            dve.wait_ge(g_tp_done, n + 1 + LOAD_CREDIT)
                            dve.wait_ge(g_ct_done, n + 1)
                            nc.vector.tensor_scalar(mask[u % 2][:, :], tp[u % 2], 0.0, MASK_ONE, ALU.not_equal,
                                                    ALU.mult).then_inc(g_m_ready, 1)
                    dve.wait_ge(g_sup_done, (s + 1) * (NB * CHAINS) + WGT_CREDIT)
                    dve.wait_ge(g_bias_added, 1)
                    base = s * G0_END
                    for k in range(SUMS):
                        sum_parts(k, acc_v, g_ln_step, base, g_acc_read, s)
                    nc.vector.tensor_tensor(strip, strip, rows_of(s), ALU.add).then_inc(g_ln_step, 1)
                    for k in range(NORM):
                        normalise(k, g_ln_step, base + SUMS, s, g_var_ready, g_root_ready, strip)
                    after(g_ln_step, base + L0_END)
                    nc.vector.tensor_scalar(rows_of(s), strip, 1.0, None, ALU.mult).then_inc(g_ln_step, 1)
                    dve.wait_ge(g_xT_done, s + 1)
                with dve.Fori(0, NS) as s:
                    with dve.Fori(0, BODIES) as g:
                        for k in range(SLOTS):
                            dve.wait_ge(g_load[k], ((s + NS) * BODIES + g + 1) * 16)
                            for t in range(TI):
                                n = ((s * BODIES + g) * SLOTS + k) * TI + t
                                dve.wait_ge(g_used, n - 1 + G_CREDIT)
                                dve.wait_ge(g_ready, n + 1 + ONE)
                                nc.vector.scalar_tensor_tensor(
                                    junk[t % 2][:, 0:CJ], acc[:, t % GRING, :], 1.0, A[k][:, t, :], ALU.mult, ALU.mult,
                                    accum_out=part[:, t, bass.ds(g * SLOTS + k, 1)]).then_inc(g_used, 1)
                    dve.wait_ge(g_used, (s + 1) * NQ * TI + G_CREDIT)
                    base = s * G1_END + NS * G0_END
                    after(g_ln_step, base)
                    nc.vector.tensor_reduce(col[0][:, :], part, AXX, ALU.add).then_inc(g_ln_step, 1)
                    for k in range(4):
                        combine(k, g_ln_step, base + 1, rows_of(s))
                    dve.wait_ge(g_out_sent, (s + 1) * 16)
                    for k in range(NORM):
                        normalise(k, g_ln_step, base + 5, s + NS, g_var_ready, g_root_ready, y[:, :, :])
                    after(g_ln_step, base + G1_END)
                    dve.sem_inc(g_y_ready, 1)
            with dve.Else():
                def body1(s, g, first, half):
                    n = s * BODIES + (0 if g is None else g)
                    for u in range(STEPS):
                        if first and u % TI == 0:
                            turn = g * (STEPS // TI) + u // TI
                            up = (BODIES - 1 - g) * (STEPS // TI) + (STEPS // TI - 1 - u // TI)
                            split(rows_of(up), 1.0 / MASK_ONE, bass.ds(up * TI, TI), pieces_step, turn,
                                  pieces_split).then_inc(pieces_ready, 1)
                            after(pieces_ready, turn + 1)
                        dve.wait_ge(m1_used, n * STEPS + u + 1)
                        unpack(u, bits[:, bass.ds(n, 1), :].rearrange("p g i -> p (g i)"), mask[u % 2], m1_ready)
                        if g is None:
                            finish1(u, s - 1, 1 - half)

                def strip1(s, half):
                    body1(s, None, False, half)
                    with dve.Fori(1, BODIES) as g:
                        body1(s, g, False, half)

                with dve.Fori(0, BODIES) as g:
                    body1(0, g, True, 0)
                with dve.Fori(0, NS // 2 - 1) as pair:
                    strip1(pair * 2 + 1, 1)
                    strip1(pair * 2 + 2, 0)
                strip1(NS - 1, 1)
                for k in range(FINISH1):
                    finish1(k, NS - 1, 1)
            dve.nop()

        @block.tensor
        def _(pe):
            pe.sem_inc(ct_done, MASK_CREDIT)
            pe.sem_inc(sup_done, WGT_CREDIT)
            pe.sem_inc(tile_done, LOAD_CREDIT)
            pe.sem_inc(m1_used, MASK_CREDIT)
            pe.sem_inc(grp_T, ONE)
            pe.sem_inc(grp_sup, ONE)
            pe.wait_ge(w_in, 16)
            pe.wait_ge(const_done, STEPS + 3)
            with pe.Fori(0, NS) as s:
                pe.wait_ge(grp_copied, s + 1 + ONE)
                pe.wait_ge(grp_Tcopied, 2 * s + ONE)
                for t in range(TI):
                    last = nc.tensor.transpose(word_half[t // 4][:, (t % 4) * P:(t % 4 + 1) * P], x_group[:, t, :],
                                               ident[:, :])
                last.then_inc(grp_T, 1)
                pe.wait_ge(grp_Tcopied, 2 * s + 2 + ONE)
                pe.wait_ge(grp_split, s + ONE)
                for t in range(TI):
                    last = nc.tensor.matmul(acc[:, 0, t * D:(t + 1) * D], x_groupT[:, t * P:(t + 1) * P], w_sb[:, :],
                                            start=True, stop=True)
                last.then_inc(grp_sup, 1)
            pe.wait_ge(support_ready, NS + ONE)

            def tile_in(v, g):
                k, tj = v // TJ, TJ - 1 - v % TJ
                if v % TJ == 0:
                    pe.wait_ge(a_load[k], (g + 1) * 16)
                if v == 0:
                    pe.wait_ge(word_read, g + ONE)
                for t in range(TI):
                    last = nc.tensor.matmul(word[:, t * P:(t + 1) * P],
                                            A_high[k][:, t, 2 * tj * P + 1:2 * (tj + 1) * P:2], bit_ident[:, v, :],
                                            start=v == 0 and t % 4 == 0, stop=True, skip_group_check=True)
                last.then_inc(tile_done, 1)

            def zero_sums(acc):
                for b in range(GRING):
                    nc.tensor.matmul(acc[:, b, 0:2 * PIECES], zeros[:, 0:P], zeros[:, 0:2 * PIECES],
                                     start=True, stop=True)

            def zero_counts():
                for c in range(CHAINS):
                    nc.tensor.matmul(count[c], zeros[:, 0:P], zeros[:, 0:HALF], start=True, stop=True)

            def counts(u, c, table):
                return nc.tensor.matmul(count[c], table[:, :], mask[u % 2][:, c * HALF:(c + 1) * HALF],
                                        start=False, stop=True, skip_group_check=True)

            def add_rows(u, down, c, lhs, acc):
                for t in range(TH):
                    i = c * TH + t
                    last = nc.tensor.matmul(acc[:, i // 2, (i % 2) * PIECES:(i % 2 + 1) * PIECES],
                                            lhs[:, t * P:(t + 1) * P], support[:, down * STEPS + (STEPS - 1 - u), :],
                                            start=False, stop=True, skip_group_check=True)
                return last

            def body0(s, g, down, first, last):
                group = s * BODIES + g
                for u in range(STEPS):
                    n = group * STEPS + u
                    pe.wait_ge(m_ready, n + 1)
                    for c in range(CHAINS):
                        counts(u, c, count_w).then_inc(v_ready, 1)
                    if u:
                        add_rows(u - 1, down, 1, wgt[1][(u - 1) % 2], acc).then_inc(sup_done, 1)
                    if not last:
                        for v in TILES_AT[u]:
                            tile_in(v, group + 1)
                    for c in range(CHAINS):
                        pe.wait_ge(w_ready, n * CHAINS + c + 1)
                        m = counts(u, c, carry_w)
                        if c == CHAINS - 1:
                            m.then_inc(ct_done, 1)
                        else:
                            if first and u == 0:
                                pe.wait_ge(acc_read, s + ONE)
                                zero_sums(acc)
                            add_rows(u, down, c, wgt[c][u % 2], acc).then_inc(sup_done, 1)
                add_rows(STEPS - 1, down, 1, wgt[1][(STEPS - 1) % 2], acc).then_inc(sup_done, 1)

            def strip0(s, last):
                zero_counts()
                body0(s, 0, BODIES - 1, True, False)
                with pe.Fori(1, BODIES - 1 if last else BODIES) as g:
                    body0(s, g, pe.snap(BODIES - 1 - g), False, False)
                if last:
                    body0(s, BODIES - 1, 0, False, True)

            for v in range(STEPS):
                tile_in(v, 0)
            with pe.Fori(0, NS - 1) as s:
                strip0(s, False)
            strip0(NS - 1, True)

            pe.wait_ge(odd_ready, 1)
            nc.tensor.matmul(count[0][0:1, 0:1], odd_sum[:, :], ones[:, :], start=True, stop=True).then_inc(odd_total, 1)
            pe.wait_ge(flag_ready, 1)
            general = pe.value_load(flag[0:1, 0:1])
            with pe.If(general != 0):
                pe.sem_inc(g_ct_done, MASK_CREDIT)
                pe.sem_inc(g_tp_done, LOAD_CREDIT)
                pe.sem_inc(g_sup_done, WGT_CREDIT)
                pe.sem_inc(g_ready, ONE)
                with pe.Fori(0, NS) as s:
                    zero_counts()
                    pe.wait_ge(g_acc_read, s + ONE)
                    zero_sums(acc)
                    with pe.Fori(0, BODIES) as g:
                        down = pe.snap(BODIES - 1 - g)
                        for u in range(STEPS):
                            k, tj = u // TJ, TJ - 1 - u % TJ
                            n = (s * BODIES + g) * STEPS + u
                            if u % TJ == 0:
                                pe.wait_ge(g_load[k], (s * BODIES + g + 1) * 16)
                            pe.wait_ge(g_m_ready, n + 1)
                            for t in range(TI):
                                last = nc.tensor.transpose(tp[u % 2][:, t * P:(t + 1) * P],
                                                           A_high[k][:, t, 2 * tj * P + 1:2 * (tj + 1) * P:2],
                                                           ident_b[:, :])
                            last.then_inc(g_tp_done, 1)
                            pe.wait_ge(g_m_ready, n + 1 + MASK_CREDIT)
                            for c in range(CHAINS):
                                counts(u, c, count_w).then_inc(g_v_ready, 1)
                            for c in range(CHAINS):
                                pe.wait_ge(g_w_ready, n * CHAINS + c + 1)
                                m = counts(u, c, carry_w)
                                if c == CHAINS - 1:
                                    m.then_inc(g_ct_done, 1)
                                add_rows(u, down, c, wgt[c][u % 2], acc).then_inc(g_sup_done, 1)
                    pe.wait_ge(g_ln_step, s * G0_END + L0_END + ONE)
                    pe.wait_ge(g_m_ready, (s + 1) * NB + MASK_CREDIT)
                    for t in range(TI):
                        last = nc.tensor.transpose(word_half[t // 4][:, (t % 4) * P:(t % 4 + 1) * P],
                                                   strip_pad[:, t, :], ident[:, :])
                    last.then_inc(g_xT_done, 1)
                    pe.wait_ge(g_xT_copied, 2 * (s + 1))
                with pe.Fori(0, NS) as s:
                    pe.wait_ge(g_xi_ready, s + 1)
                    pe.sem_inc(product_turn, 1)
                    with pe.Fori(0, BODIES) as g:
                        down = pe.snap(BODIES - 1 - g)
                        for k in range(SLOTS):
                            j0 = down * (SLOTS * CJ) + (SLOTS - 1 - k) * CJ
                            for t in range(TI):
                                n = ((s * BODIES + g) * SLOTS + k) * TI + t
                                pe.wait_ge(g_used, n + 1 + G_CREDIT - GRING)
                                pe.sem_inc(product_turn, 1)
                                nc.tensor.matmul(acc[:, t % GRING, :], x_groupT[:, t * P:(t + 1) * P],
                                                 xT[:, bass.ds(j0, CJ)], start=True, stop=True).then_inc(g_ready, 1)
            with pe.Else():
                with pe.Fori(0, NS // 2) as pair:
                    for half in range(2):
                        s = pair * 2 + half
                        pe.wait_ge(acc_read, s + NS)
                        zero_sums(sums[half])
                        with pe.Fori(0, BODIES) as g:
                            down = pe.snap(BODIES - 1 - g)
                            for u in range(STEPS):
                                if u % TI == 0:
                                    pe.wait_ge(pieces_ready, g * (STEPS // TI) + u // TI + 1 + ONE)
                                pe.wait_ge(m1_ready, (s * BODIES + g) * STEPS + u + 1)
                                if u == 0:
                                    pe.sem_inc(product_turn, 1)
                                add_rows(u, down, 0, mask[u % 2], sums[half])
                                add_rows(u, down, 1, mask[u % 2][:, HALF:STRIP], sums[half]).then_inc(m1_used, 1)
            pe.nop()


_INS = ['x', 'adj', 'L0_gnn_weight', 'L0_gnn_bias']
_OUTS = [((8192, 64), 'float32')]


def kernel(**inputs):
    import numpy as _np
    import concourse.bacc as _bacc
    from concourse import mybir as _mybir
    from concourse.bass_utils import run_bass_kernel_spmd as _run

    nc = _bacc.Bacc("TRN2", target_bir_lowering=False, num_devices=1)
    arrays, args = {}, []
    for name in _INS:
        a = _np.ascontiguousarray(inputs[name])
        arrays[f"in_{name}_dram"] = a
        args.append(nc.dram_tensor(f"in_{name}_dram", a.shape, _mybir.dt.from_np(a.dtype), kind="ExternalInput").ap())
    for i, (shape, dtype) in enumerate(_OUTS):
        dt = _mybir.dt.from_np(_np.dtype(dtype))
        args.append(nc.dram_tensor(f"out_{i}_dram", shape, dt, kind="ExternalOutput").ap())
    adj_resnorm_kernel(nc, *args)
    r = _run(nc, [arrays], core_ids=[0])
    got = tuple(r.results[0][f"out_{i}_dram"] for i in range(len(_OUTS)))
    return got[0]
```

```python
from contextlib import ExitStack

import concourse.bass as bass
from concourse import mybir

ALU = mybir.AluOpType
ACT = mybir.ActivationFunctionType
AXX = mybir.AxisListType.X
F32 = mybir.dt.float32
BF16 = mybir.dt.bfloat16
F16 = mybir.dt.float16
I16 = mybir.dt.int16
U16 = mybir.dt.uint16
I32 = mybir.dt.int32

P = 128
MAX_NEIGH = 100
EPS = 1e-5
F_CONST, B_CONST, R_CONST = 1.0, 0.1, 0.01
WEIGHT_SHIFT = 2.0 ** (127 - MAX_NEIGH)
SUPPORT_SCALE = 2.0 ** 9
RANGE = 4e9
ROW_SCALE = 2.0 ** 12
BF16_EXPONENT_STEP = 128.0


def adj_resnorm_kernel(nc, x, adj, weight, bias, out):
    N, D = x.shape
    NB = N // P
    TI = 8
    STRIP = TI * P
    NS = N // STRIP
    CJ = 512
    NQ = N // CJ
    TJ = CJ // P
    SLOTS = 4
    STEPS = SLOTS * TJ
    BODIES = NB // STEPS
    GROUPS = NS * BODIES
    CHAINS = 2
    HALF = STRIP // CHAINS
    TH = HALF // P
    PIECES = 2 * D
    G_PIECES = 3 * D
    GRING = 4
    ONE_BIT = 14
    MASK_ONE = 2.0
    MASKS = 8
    AHEAD = 2
    PAIRS = TI // 2

    adj_v = adj.rearrange("(s t p) j -> s p t j", t=TI, p=P)
    x_v = x.rearrange("(b p) d -> p b d", p=P)
    out_v = out.rearrange("(s t p) d -> s p t d", t=TI, p=P)

    ctx = ExitStack()
    with ctx:
        def sb(name, shape, dt):
            return ctx.enter_context(nc.sbuf_tensor(name, shape, dt))

        def pb(name, shape, dt):
            return ctx.enter_context(nc.psum_tensor(name, shape, dt))

        def sem(name):
            return ctx.enter_context(nc.semaphore(name))

        A = [sb(f"A{k}", [P, TI, CJ], F32) for k in range(SLOTS)]
        A_high = [a[:, :, :].bitcast(BF16) for a in A]
        bits = sb("bits", [P, GROUPS, STRIP], U16)
        x_all = sb("x_all", [P, NB, D], F32)
        w_pair = sb("w_pair", [P, 2 * D], F32)
        bias_sb = sb("bias_sb", [P, D], F32)
        support = sb("support", [P, NB, PIECES], F16)
        y = sb("y", [P, TI, D], F32)
        square = sb("square", [P, TI, D], F32)
        rest = [y, square]
        x_groupT = sb("x_groupT", [P, STRIP], F32)
        sums_sb = x_groupT
        fold = sb("fold", [P, D], F32)
        ident = sb("ident", [P, P], F32)
        ident_b = sb("ident_b", [P, P], BF16)
        bit_ident = sb("bit_ident", [P, STEPS, P], BF16)
        count_w = sb("count_w", [P, P], BF16)
        carry_w = sb("carry_w", [P, P], BF16)
        zeros = sb("zeros", [P, 512], BF16)
        ones = sb("ones", [P, 1], F32)
        mask = [sb(f"mask{k}", [P, STRIP], BF16) for k in range(MASKS)]
        wgt = [[sb(f"wgt{c}{k}", [P, HALF], BF16) for k in range(2)] for c in range(CHAINS)]
        strip_pad = sb("strip_pad", [P, TI, P], F32)
        strip = strip_pad[:, :, 0:D]
        junk = [sb(f"junk{k}", [P, STRIP], BF16) for k in range(2)]
        odd = sb("odd", [P, GROUPS * STEPS + NS], F32)
        scaled = [j[:, :].bitcast(F32).rearrange("p (t d) -> p t d", d=D) for j in junk]
        odd_sum = sb("odd_sum", [P, 1], F32)
        flag = sb("flag", [1, 1], I32)
        minus_half = sb("minus_half", [P, TI], F32)
        col = [sb(f"col{k}", [P, TI], F32) for k in range(4)]

        xT = bits[:, 0:2 * NS, :].rearrange("p g i -> p (g i)").bitcast(F32)
        part = bits[:, 2 * NS, 0:2 * TI * NQ].bitcast(F32).rearrange("p (t q) -> p t q", q=NQ)
        g_support = bits[:, 2 * NS + 1:2 * NS + 1 + NB * G_PIECES // STRIP, :].rearrange(
            "p g i -> p (g i)").bitcast(BF16).rearrange("p (b c) -> p b c", c=G_PIECES)

        banks = pb("banks", [P, 2 * GRING, 512], F32)
        sums = banks[:, 0:CHAINS, :]
        sums1 = [banks[:, GRING + 2 * k:GRING + 2 * k + 2, :] for k in range(2)]
        turned = [banks[:, 2 + k, :].rearrange("p (t d) -> p t d", d=D) for k in range(2)]
        g_acc = banks[:, 0:GRING, :]
        g_acc_v = g_acc[:, :, 0:2 * G_PIECES].rearrange("p b (h c) -> p b h c", h=2)
        count = [banks[:, GRING + c, :] for c in range(CHAINS)]
        word_half = [banks[:, GRING + CHAINS + k, :] for k in range(2)]
        word = banks[:, GRING + CHAINS:GRING + CHAINS + 2, :].rearrange("p b i -> p (b i)")
        tp = [w.bitcast(BF16) for w in word_half]
        strip_h = strip.rearrange("p (b h) d -> p b h d", h=2)
        products = [banks[:, k, :].rearrange("p (t d) -> p t d", d=D) for k in range(2)]

        X_LOADS = NS // 2
        x_in = [sem(f"x_in{k}") for k in range(X_LOADS)]
        w_in, b_in, const_set, const_done = (sem(n) for n in ("w_in", "b_in", "const_set", "const_done"))
        ident_ready, w_ready_pair, bits_ready = (sem(n) for n in ("ident_ready", "w_ready_pair", "bits_ready"))
        grp_T, grp_Tcopied, grp_sup = (sem(n) for n in ("grp_T", "grp_Tcopied", "grp_sup"))
        high_ready, pieces_ready, squares_ready = (sem(n) for n in ("high_ready", "pieces_ready", "squares_ready"))
        bias_added, w_zeroed = (sem(n) for n in ("bias_added", "w_zeroed"))
        load_turn = sem("load_turn")
        product_turn = sem("product_turn")
        a_load = [sem(f"a_load{k}") for k in range(SLOTS)]
        tile_done, tile_tested, word_read = (sem(n) for n in ("tile_done", "tile_tested", "word_read"))
        m_ready, ct_done, v_ready, w_ready, sup_done, acc_read = (
            sem(n) for n in ("m_ready", "ct_done", "v_ready", "w_ready", "sup_done", "acc_read"))
        ln_step, var_ready, root_ready = (sem(n) for n in ("ln_step", "var_ready", "root_ready"))
        odd_ready, odd_total, flag_ready = (sem(n) for n in ("odd_ready", "odd_total", "flag_ready"))
        m1_ready, m1_used, ln1_step = (sem(n) for n in ("m1_ready", "m1_used", "ln1_step"))
        y_ready, out_sent = sem("y_ready"), sem("out_sent")
        base_ready, scaled_ready = sem("base_ready"), sem("scaled_ready")
        fold_ready, turned_ready = sem("fold_ready"), sem("turned_ready")
        ends_turn, rows_turn = sem("ends_turn"), sem("rows_turn")
        g_load = [sem(f"g_load{k}") for k in range(SLOTS)]
        (g_x_in, g_bias_added, g_tp_done, g_m_ready, g_ct_done, g_v_ready, g_w_ready, g_sup_done, g_acc_read,
         g_ln_step, g_var_ready, g_root_ready, g_xT_done, g_xT_copied, g_xi_ready, g_ready, g_used, g_y_ready,
         g_out_sent, g_w_ready_pair, g_T, g_Tcopied, g_sup, g_high_ready, g_rest_ready, g_mid_ready,
         g_pieces_ready) = (sem("g_" + n) for n in (
             "x_in", "bias_added", "tp_done", "m_ready", "ct_done", "v_ready", "w_ready", "sup_done", "acc_read",
             "ln_step", "var_ready", "root_ready", "xT_done", "xT_copied", "xi_ready", "ready", "used", "y_ready",
             "out_sent", "w_ready_pair", "T", "Tcopied", "sup", "high_ready", "rest_ready", "mid_ready",
             "pieces_ready"))

        block = ctx.enter_context(nc.Block())

        LOAD_CREDIT = STEPS
        G_MASK_CREDIT = 2
        WGT_CREDIT = 2 * CHAINS
        G_CREDIT = SLOTS * TI
        ONE = 1

        SUMS, G_SUMS, NORM = 2, 3, 7
        L0_END = (SUMS - 1) + 1 + (NORM - 1)
        L1_END = (SUMS - 1) + 2 + 3 + (NORM - 1)
        G0_END, G1_END = (G_SUMS - 1) + 1 + (NORM - 1) + 1, 1 + 4 + (NORM - 1)
        FINISH0, FINISH1 = SUMS + 1 + NORM, SUMS + 2 + 3 + NORM
        WORDS_AT = STEPS - AHEAD

        END_STEPS = [7, 13, 15, 20, 26, 32, 34, 39, 44, 48, 51, 62]
        ENDS_AT = {step: (SUMS + k,) for k, step in enumerate(END_STEPS)}
        TURN_AT0, TURN_AT1 = 2, 4
        ENDS0 = {3 * k: (SUMS - 1 + k,) for k in range(1, FINISH0 - SUMS + 1)}
        ENDS0[0] = tuple(range(SUMS))
        ENDS0_AT = {2 + 3 * k: (k,) for k in range(SUMS, FINISH0 - 1)}
        ENDS0_AT[0] = tuple(range(SUMS))
        ENDS0_AT[2 + 3 * FINISH0] = (FINISH0 - 1,)

        def across(c):
            return c[:, :].unsqueeze(2).to_broadcast([P, TI, D])

        @block.sync
        def _(sp):
            for k in range(X_LOADS):
                blocks = slice(k * NB // X_LOADS, (k + 1) * NB // X_LOADS)
                sp.dma_start(x_all[:, blocks, :], x_v[:, blocks, :]).then_inc(x_in[k], 16)
                if k == 0:
                    sp.wait_ge(w_zeroed, 1)
                    for h in range(2):
                        sp.dma_start(w_pair[h * D:(h + 1) * D, h * D:(h + 1) * D], weight).then_inc(w_in, 16)
            sp.dma_start(bias_sb[:, :], bias.partition_broadcast(P)).then_inc(b_in, 16)
            with sp.Fori(0, NS) as s:
                with sp.Fori(0, BODIES) as g:
                    down = sp.snap(BODIES - 1 - g)
                    for k in range(SLOTS):
                        j0 = down * (SLOTS * CJ) + (SLOTS - 1 - k) * CJ
                        used = (s * BODIES + g) * STEPS + (k + 1) * TJ
                        sp.wait_ge(tile_tested, used)
                        sp.wait_ge(tile_done, used)
                        sp.sem_inc(load_turn, 1)
                        sp.dma_start(A[k][:, :, :], adj_v[s, :, :, bass.ds(j0, CJ)]).then_inc(a_load[k], 16)
            sp.wait_ge(flag_ready, 1)
            general = sp.value_load(flag[0:1, 0:1])
            with sp.If(general != 0):
                sp.wait_ge(ln_step, NS * L0_END + ONE)
                sp.dma_start(x_all[:, :, :], x_v).then_inc(g_x_in, 16)
                with sp.Fori(0, NS) as s:
                    with sp.Fori(0, BODIES) as g:
                        down = sp.snap(BODIES - 1 - g)
                        for k in range(SLOTS):
                            j0 = down * (SLOTS * CJ) + (SLOTS - 1 - k) * CJ
                            sp.wait_ge(g_tp_done, (s * BODIES + g) * STEPS + (k + 1) * TJ)
                            sp.sem_inc(load_turn, 1)
                            sp.dma_start(A[k][:, :, :], adj_v[s, :, :, bass.ds(j0, CJ)]).then_inc(g_load[k], 16)
                sp.wait_ge(g_tp_done, LOAD_CREDIT + NS * NB)
                with sp.Fori(0, NS) as s:
                    with sp.Fori(0, BODIES) as g:
                        down = sp.snap(BODIES - 1 - g)
                        for k in range(SLOTS):
                            j0 = down * (SLOTS * CJ) + (SLOTS - 1 - k) * CJ
                            sp.wait_ge(g_used, (s * BODIES + g) * SLOTS * TI + (k + 1) * TI)
                            sp.sem_inc(load_turn, 1)
                            sp.dma_start(A[k][:, :, :], adj_v[s, :, :, bass.ds(j0, CJ)]).then_inc(g_load[k], 16)
                sp.wait_ge(g_out_sent, 16 * (NS + 1))
            with sp.Else():
                with sp.Fori(0, NS) as s:
                    sp.wait_ge(y_ready, s + 1)
                    sp.sem_inc(load_turn, 1)
                    sp.dma_start(out_v[s], y[:, :, :]).then_inc(out_sent, 16)
                sp.wait_ge(out_sent, 16 * (NS + 1))
            sp.nop()

        @block.gpsimd
        def _(pool):
            pool.memset(w_pair[:, :], 0.0).then_inc(w_zeroed, 1)
            pool.memset(ident[:, :], 0.0).then_inc(const_set, 1)
            pool.wait_ge(const_set, 1)
            pool.affine_select(out=ident[:, :], in_=ident[:, :], compare_op=ALU.not_equal, fill=1.0,
                               base=0, pattern=[[-1, P]], channel_multiplier=1).then_inc(ident_ready, 1)
            pool.wait_ge(ident_ready, 1)
            pool.tensor_tensor(fold[:, :], ident[:, 0:D], ident[:, D:2 * D], ALU.add).then_inc(fold_ready, 1)
            pool.memset(zeros[:, :], 0.0).then_inc(const_done, 1)
            pool.memset(ones[:, :], 1.0).then_inc(const_done, 1)
            pool.memset(minus_half[:, :], -0.5).then_inc(const_set, 1)
            pool.memset(count_w[:, :], -1.0 / MASK_ONE).then_inc(const_set, 1)
            pool.memset(carry_w[:, :], -1.0 / MASK_ONE).then_inc(const_set, 1)
            pool.wait_ge(w_in, 32)
            pool.tensor_scalar(w_pair[:, :], w_pair[:, :], SUPPORT_SCALE, None, ALU.mult).then_inc(w_ready_pair, 1)
            pool.wait_ge(const_set, 4)
            pool.affine_select(out=count_w[:, :], in_=count_w[:, :], compare_op=ALU.is_ge, fill=0.0,
                               base=0, pattern=[[-1, P]], channel_multiplier=1).then_inc(const_set, 1)
            pool.affine_select(out=carry_w[:, :], in_=carry_w[:, :], compare_op=ALU.is_ge, fill=0.0,
                               base=0, pattern=[[1, P]], channel_multiplier=-1).then_inc(const_set, 1)
            pool.wait_ge(const_set, 6)
            pool.affine_select(out=count_w[:, :], in_=count_w[:, :], compare_op=ALU.not_equal,
                               fill=MAX_NEIGH / MASK_ONE, base=0, pattern=[[-1, P]],
                               channel_multiplier=1).then_inc(const_done, 1)
            pool.affine_select(out=carry_w[:, :], in_=carry_w[:, :], compare_op=ALU.not_equal,
                               fill=(-1 - MAX_NEIGH) / MASK_ONE, base=0, pattern=[[-1, P]],
                               channel_multiplier=1).then_inc(const_done, 1)
            pool.memset(strip_pad[:, :, :], 0.0).then_inc(const_done, 1)
            pool.wait_ge(b_in, 16)
            pool.wait_ge(grp_T, NS)
            pool.tensor_tensor(x_all[:, :, :], x_all[:, :, :],
                               bias_sb[:, :].unsqueeze(1).to_broadcast([P, NB, D]), ALU.add).then_inc(bias_added, 1)

            def root(ready, n, done):
                pool.wait_ge(ready, n + 1)
                pool.tensor_tensor(col[3][:, :], col[2][:, :], minus_half[:, :], ALU.pow).then_inc(done, 1)

            with pool.Fori(0, NS - 1) as s:
                root(var_ready, s, root_ready)
            pool.wait_ge(flag_ready, 1)
            general = pool.value_load(flag[0:1, 0:1])
            with pool.If(general != 0):
                root(var_ready, NS - 1, root_ready)
                pool.tensor_scalar(w_pair[:, :], w_pair[:, :], WEIGHT_SHIFT / SUPPORT_SCALE, None,
                                   ALU.mult).then_inc(g_w_ready_pair, 1)
                pool.wait_ge(g_x_in, 16)
                pool.wait_ge(g_T, NS)
                pool.tensor_tensor(x_all[:, :, :], x_all[:, :, :], bias_sb[:, :].unsqueeze(1).to_broadcast([P, NB, D]),
                                   ALU.add).then_inc(g_bias_added, 1)
                with pool.Fori(0, 2 * NS) as s:
                    root(g_var_ready, s, g_root_ready)
            with pool.Else():
                def low_rows(s, k):
                    pool.wait_ge(scaled_ready, s + 1)
                    pool.wait_ge(high_ready, s + NS + 1)
                    pool.sem_inc(rows_turn, 1)
                    blocks = bass.ds(s * TI, TI)
                    pool.tensor_tensor(support[:, blocks, D:2 * D], scaled[k], support[:, blocks, 0:D],
                                       ALU.subtract).then_inc(pieces_ready, 1)

                with pool.Fori(0, NS // 2 - 1) as pair:
                    for k in range(2):
                        low_rows(pair * 2 + k, k)
                low_rows(NS - 2, 0)
                root(var_ready, NS - 1, root_ready)
                low_rows(NS - 1, 1)
                with pool.Fori(NS, 2 * NS) as s:
                    root(var_ready, s, root_ready)
            pool.nop()

        @block.scalar
        def _(act):
            def transposed(s, T, copied, sup):
                act.wait_ge(T, s + 1)
                if s >= 2:
                    act.wait_ge(sup, s - 1)
                nc.scalar.copy(x_groupT[:, s % 2 * 512:(s % 2 + 1) * 512], word_half[s % 2]).then_inc(copied, 1)

            act.wait_ge(ident_ready, 1)
            nc.scalar.activation(ident_b[:, :], ident[:, :], ACT.Relu).then_inc(const_done, 1)
            for s in range(NS + 1):
                if s < NS:
                    transposed(s, grp_T, grp_Tcopied, grp_sup)
                if s:
                    act.wait_ge(grp_sup, s)
                    nc.scalar.copy(support[:, (s - 1) * TI:s * TI, 0:D], products[(s - 1) % 2]).then_inc(high_ready, 1)
                    act.wait_ge(high_ready, s)
                    if s > 1:
                        act.wait_ge(squares_ready, s - 1)
                    nc.scalar.activation(square[:, :, :], support[:, (s - 1) * TI:s * TI, 0:D], ACT.Square,
                                         accum_out=odd[:, NS * NB + s - 1:NS * NB + s]).then_inc(squares_ready, 1)

            def weights(u, n, counted, used, ready):
                for c in range(CHAINS):
                    act.wait_ge(counted, n * CHAINS + c + 1)
                    act.wait_ge(used, n * CHAINS + c + 1)
                    nc.scalar.activation(wgt[c][u % 2][:, :].bitcast(I16), count[c][:, :], ACT.Relu,
                                         scale=BF16_EXPONENT_STEP).then_inc(ready, 1)

            with act.Fori(0, GROUPS) as g:
                for u in range(STEPS):
                    weights(u, g * STEPS + u, v_ready, sup_done, w_ready)
            act.wait_ge(flag_ready, 1)
            general = act.value_load(flag[0:1, 0:1])
            with act.If(general != 0):
                for s in range(NS):
                    blocks = slice(s * TI, (s + 1) * TI)
                    transposed(s, g_T, g_Tcopied, g_sup)
                    act.wait_ge(g_sup, s + 1)
                    nc.scalar.copy(g_support[:, blocks, 0:D], products[s % 2]).then_inc(g_high_ready, 1)
                    act.wait_ge(g_rest_ready, s + 1)
                    nc.scalar.copy(g_support[:, blocks, D:2 * D], rest[s % 2][:, :, :]).then_inc(g_mid_ready, 1)
                with act.Fori(0, NS) as s:
                    with act.Fori(0, BODIES) as g:
                        for u in range(STEPS):
                            weights(u, (s * BODIES + g) * STEPS + u, g_v_ready, g_sup_done, g_w_ready)
                    act.wait_ge(g_xT_done, s + 1)
                    for k in range(2):
                        nc.scalar.copy(xT[:, bass.ds(s * STRIP + k * 512, 512)],
                                       word_half[k]).then_inc(g_xT_copied, 1)
                act.wait_ge(g_xT_copied, 2 * NS)
                with act.Fori(0, NS) as s:
                    act.wait_ge(g_ready, s * (NQ * TI) + ONE)
                    nc.scalar.copy(x_groupT[:, :], xT[:, bass.ds(s * STRIP, STRIP)]).then_inc(g_xi_ready, 1)
                    act.wait_ge(g_y_ready, s + 1)
                    act.dma_start(out_v[s], y[:, :, :]).then_inc(g_out_sent, 16)
            with act.Else():
                with act.Fori(0, NS // 2) as pair:
                    for k in range(2):
                        s = pair * 2 + k
                        rows = x_all[:, bass.ds(s * TI, TI), :]
                        act.wait_ge(ln_step, (s + 1) * L0_END + ONE)
                        act.wait_ge(pieces_ready, s + NS - 1)
                        act.sem_inc(ends_turn, 1)
                        nc.scalar.activation(scaled[k], rows, ACT.Copy, scale=ROW_SCALE).then_inc(scaled_ready, 1)
                        act.wait_ge(sup_done, GROUPS * STEPS * CHAINS + WGT_CREDIT)
                        nc.scalar.activation(support[:, bass.ds(s * TI, TI), 0:D], rows, ACT.Copy,
                                             scale=ROW_SCALE).then_inc(high_ready, 1)
                with act.Fori(0, NS // 2) as pair:
                    for turn in range(2):
                        s = pair * 2 + turn
                        base = s * L1_END
                        act.wait_ge(ln1_step, base + ONE)
                        act.wait_ge(m1_used, (s + 1) * NB + MASKS)
                        nc.scalar.copy(sums_sb[:, 0:HALF], sums1[turn][:, 0, :]).then_inc(ln1_step, 1)
                        nc.scalar.copy(sums_sb[:, HALF:STRIP], sums1[turn][:, 1, :]).then_inc(acc_read, 1)
                        act.wait_ge(ln1_step, base + SUMS + ONE)
                        act.sem_inc(ends_turn, 1)
                        nc.scalar.activation(strip, x_all[:, bass.ds(s * TI, TI), :], ACT.Copy, bias=F_CONST,
                                             scale=-B_CONST).then_inc(base_ready, 1)
                        act.wait_ge(ln1_step, base + SUMS + 4 + 3 + ONE)
                        nc.scalar.activation(square[:, :, :], strip, ACT.Square).then_inc(ln1_step, 1)
            act.nop()

        @block.vector
        def _(dve):
            dve.sem_inc(acc_read, ONE)
            dve.sem_inc(word_read, ONE)
            dve.sem_inc(tile_tested, LOAD_CREDIT)
            for step in (ln_step, ln1_step):
                dve.sem_inc(step, ONE)
            dve.sem_inc(out_sent, 16)
            dve.wait_ge(ident_ready, 1)
            for v in range(STEPS):
                nc.vector.tensor_scalar(bit_ident[:, v, :], ident[:, :], float(1 << v), None,
                                        ALU.mult).then_inc(bits_ready, 1)

            def after(step, n):
                dve.wait_ge(step, n + ONE)

            def low_part(src, scale, blocks, turn):
                dve.wait_ge(high_ready, turn + 1)
                nc.vector.scalar_tensor_tensor(support[:, blocks, D:2 * D], src, scale, support[:, blocks, 0:D],
                                               ALU.mult, ALU.subtract).then_inc(pieces_ready, 1)

            def copy_sums(k, base, turn):
                after(ln_step, base + k)
                nc.vector.tensor_scalar(sums_sb[:, k * HALF:(k + 1) * HALF], sums[:, k, :], 1.0, None,
                                        ALU.mult).then_inc(ln_step if k == 0 else acc_read, 1)
                if k:
                    after(acc_read, turn + 1)

            def g_sum_parts(k, step, base, read, turn):
                after(step, base + k)
                if k == 0:
                    nc.vector.tensor_scalar(strip_h, g_acc_v[:, :, :, 2 * D:3 * D], 1.0, None,
                                            ALU.mult).then_inc(step, 1)
                elif k == 1:
                    nc.vector.tensor_tensor(strip_h, strip_h, g_acc_v[:, :, :, D:2 * D], ALU.add).then_inc(step, 1)
                else:
                    nc.vector.tensor_tensor(strip_h, strip_h, g_acc_v[:, :, :, 0:D], ALU.add).then_inc(read, 1)
                    after(read, turn + 1)

            def normalise(k, step, base, n, ready, done, dst):
                total, mean, var, inv = col
                if k != NORM - 1:
                    after(step, base + k)
                if k == 0:
                    nc.vector.tensor_reduce(total[:, :], strip, AXX, ALU.add).then_inc(step, 1)
                elif k == 1:
                    nc.vector.tensor_scalar(mean[:, :], total[:, :], 1.0 / D, None, ALU.mult).then_inc(step, 1)
                elif k == 2:
                    nc.vector.tensor_tensor(strip, strip, across(mean), ALU.subtract).then_inc(step, 1)
                elif k == 3:
                    nc.vector.tensor_tensor(square[:, :, :], strip, strip, ALU.mult).then_inc(step, 1)
                elif k == 4:
                    nc.vector.tensor_reduce(total[:, :], square[:, :, :], AXX, ALU.add).then_inc(step, 1)
                elif k == 5:
                    nc.vector.tensor_scalar(var[:, :], total[:, :], 1.0 / D, EPS, ALU.mult, ALU.add).then_inc(ready, 1)
                else:
                    dve.wait_ge(done, n + 1)
                    nc.vector.tensor_tensor(dst, strip, across(inv), ALU.mult).then_inc(step, 1)

            def combine(k, step, base, rows, factor):
                outer = col[0]
                if k != 1:
                    after(step, base + k)
                if k == 0:
                    nc.vector.tensor_scalar(outer[:, :], outer[:, :], factor, None, ALU.mult).then_inc(step, 1)
                elif k == 1:
                    nc.vector.tensor_scalar(strip, rows, -B_CONST, F_CONST, ALU.mult, ALU.add).then_inc(step, 1)
                elif k == 2:
                    nc.vector.tensor_tensor(strip, strip, across(outer), ALU.subtract).then_inc(step, 1)
                else:
                    nc.vector.tensor_tensor(strip, strip, rows, ALU.add).then_inc(step, 1)

            def rows_of(s):
                return x_all[:, bass.ds(s * TI, TI), :]

            def finish0(k, s):
                base = s * L0_END
                if k == 0:
                    dve.wait_ge(sup_done, (s + 1) * (NB * CHAINS) + WGT_CREDIT)
                    dve.wait_ge(bias_added, 1)
                if k < SUMS:
                    copy_sums(k, base, s)
                elif k == SUMS:
                    dve.wait_ge(turned_ready, s + 2)
                    nc.vector.scalar_tensor_tensor(strip, turned[0], WEIGHT_SHIFT / SUPPORT_SCALE, rows_of(s),
                                                   ALU.mult, ALU.add).then_inc(ln_step, 1)
                else:
                    normalise(k - SUMS - 1, ln_step, base + SUMS, s, var_ready, root_ready, rows_of(s))

            def finish1(k, s, half):
                base = s * L1_END
                if k < SUMS:
                    return
                if k == SUMS:
                    dve.wait_ge(turned_ready, s + NS + 2)
                    nc.vector.scalar_tensor_tensor(square[:, :, :], turned[half], 1.0 / (MASK_ONE * ROW_SCALE),
                                                   rows_of(s), ALU.mult, ALU.mult).then_inc(ln1_step, 1)
                elif k == SUMS + 1:
                    after(ln1_step, base + SUMS)
                    nc.vector.tensor_reduce(col[0][:, :], square[:, :, :], AXX, ALU.add).then_inc(ln1_step, 1)
                elif k == SUMS + 2:
                    combine(0, ln1_step, base + SUMS + 1, None, R_CONST)
                elif k == SUMS + 3:
                    dve.wait_ge(base_ready, s + 1)
                    combine(2, ln1_step, base + SUMS, None, R_CONST)
                elif k == SUMS + 4:
                    combine(3, ln1_step, base + SUMS, rows_of(s), R_CONST)
                else:
                    n = k - SUMS - 5
                    if n == 3:
                        return
                    if n == NORM - 1:
                        dve.wait_ge(out_sent, (s + 1) * 16)
                    normalise(n, ln1_step, base + SUMS + 4, s + NS, var_ready, root_ready, y[:, :, :])
                    if n == NORM - 1:
                        after(ln1_step, base + L1_END)
                        dve.sem_inc(y_ready, 1)

            def unpack(u, word16, dst, ready):
                if u <= ONE_BIT:
                    ops = (ONE_BIT - u, 1 << ONE_BIT, ALU.logical_shift_left, ALU.bitwise_and)
                else:
                    ops = (u - ONE_BIT, 1 << ONE_BIT, ALU.logical_shift_right, ALU.bitwise_and)
                nc.vector.tensor_scalar(dst[:, :].bitcast(U16), word16, *ops).then_inc(ready, 1)

            def next_mask(u, g):
                dve.wait_ge(ct_done, g * STEPS + u + 1)
                unpack(u, bits[:, bass.ds(g, 1), :].rearrange("p g i -> p (g i)"), mask[u % MASKS], m_ready)

            def read_words(g):
                dve.wait_ge(tile_done, (g + 1) * STEPS + LOAD_CREDIT)
                nc.vector.tensor_scalar(bits[:, bass.ds(g, 1), :].rearrange("p g i -> p (g i)"), word[:, :], 1.0, None,
                                        ALU.mult).then_inc(word_read, 1)
                dve.wait_ge(word_read, g + 1 + ONE)

            def test(u, g):
                k, tj = u // TJ, TJ - 1 - u % TJ
                if u % TJ == 0:
                    dve.wait_ge(a_load[k], (g + 1) * 16)
                tile = A[k][:, :, tj * P:(tj + 1) * P]
                dve.wait_ge(tile_tested, g * STEPS + u - 1 + LOAD_CREDIT)
                nc.vector.scalar_tensor_tensor(junk[u % 2][:, :].rearrange("p (t j) -> p t j", t=TI), tile, 1.0, tile,
                                               ALU.is_equal, ALU.not_equal,
                                               accum_out=odd[:, bass.ds(g * STEPS + u, 1)]).then_inc(tile_tested, 1)

            def body0(s, g, ends_at, last=False):
                n = s * BODIES + g
                for u in range(STEPS):
                    if not last and u == WORDS_AT:
                        read_words(n + 1)
                    if u + AHEAD < STEPS:
                        next_mask(u + AHEAD, n)
                    elif not last:
                        next_mask(u + AHEAD - STEPS, n + 1)
                    for k in ends_at.get(u, ()):
                        finish0(k, s - 1)
                    if not last:
                        test(u, n + 1)

            for s in range(NS):
                low_part(products[s % 2], 1.0, slice(s * TI, (s + 1) * TI), s)
                if s >= NS - TJ:
                    test(s - (NS - TJ), 0)
            for u in range(TJ, STEPS - TJ):
                test(u, 0)
            read_words(0)
            for u in range(AHEAD):
                next_mask(u, 0)
            for u in range(STEPS - TJ, STEPS):
                test(u, 0)
            dve.wait_ge(squares_ready, NS)
            nc.vector.tensor_scalar(odd[:, NS * NB:], odd[:, NS * NB:], RANGE, None, ALU.is_gt).then_inc(squares_ready, 1)
            ends = [{u: ENDS0[g * STEPS + u] for u in range(STEPS) if g * STEPS + u in ENDS0} for g in range(2)]
            with dve.Fori(0, BODIES) as g:
                body0(0, g, {})
            with dve.Fori(1, NS - 1) as s:
                for g in range(2):
                    body0(s, g, ends[g])
                with dve.Fori(2, BODIES) as g:
                    body0(s, g, {})
            for g in range(2):
                body0(NS - 1, g, ends[g])
            with dve.Fori(2, BODIES - 1) as g:
                body0(NS - 1, g, {})
            dve.wait_ge(tile_tested, NS * NB + LOAD_CREDIT)
            dve.wait_ge(squares_ready, NS + 1)
            nc.vector.tensor_reduce(odd_sum[:, :], odd[:, :], AXX, ALU.add).then_inc(odd_ready, 1)
            body0(NS - 1, BODIES - 1, {}, True)
            dve.wait_ge(odd_total, 1)
            nc.vector.tensor_copy(flag[:, :], word[0:1, 0:1]).then_inc(flag_ready, 1)
            dve.wait_ge(flag_ready, 1)
            general = dve.value_load(flag[0:1, 0:1])
            with dve.If(general != 0):
                for k in range(FINISH0):
                    finish0(k, NS - 1)
                after(ln_step, NS * L0_END)
                for s in range(NS):
                    blocks = slice(s * TI, (s + 1) * TI)
                    dve.wait_ge(g_high_ready, s + 1)
                    nc.vector.tensor_tensor(rest[s % 2][:, :, :], products[s % 2], g_support[:, blocks, 0:D],
                                            ALU.subtract).then_inc(g_rest_ready, 1)
                    dve.wait_ge(g_mid_ready, s + 1)
                    dve.wait_ge(g_rest_ready, s + 1)
                    nc.vector.tensor_tensor(g_support[:, blocks, 2 * D:3 * D], rest[s % 2][:, :, :],
                                            g_support[:, blocks, D:2 * D], ALU.subtract).then_inc(g_pieces_ready, 1)
                dve.sem_inc(g_m_ready, G_MASK_CREDIT)
                dve.sem_inc(g_used, G_CREDIT)
                dve.sem_inc(g_out_sent, 16)
                dve.sem_inc(g_acc_read, ONE)
                dve.sem_inc(g_ln_step, ONE)
                with dve.Fori(0, NS) as s:
                    with dve.Fori(0, BODIES) as g:
                        for u in range(STEPS):
                            n = s * NB + g * STEPS + u
                            dve.wait_ge(g_tp_done, n + 1 + LOAD_CREDIT)
                            dve.wait_ge(g_ct_done, n + 1)
                            nc.vector.tensor_scalar(mask[u % 2][:, :], tp[u % 2], 0.0, MASK_ONE, ALU.not_equal,
                                                    ALU.mult).then_inc(g_m_ready, 1)
                    dve.wait_ge(g_sup_done, (s + 1) * (NB * CHAINS) + WGT_CREDIT)
                    dve.wait_ge(g_bias_added, 1)
                    base = s * G0_END
                    for k in range(G_SUMS):
                        g_sum_parts(k, g_ln_step, base, g_acc_read, s)
                    nc.vector.tensor_tensor(strip, strip, rows_of(s), ALU.add).then_inc(g_ln_step, 1)
                    for k in range(NORM):
                        normalise(k, g_ln_step, base + G_SUMS, s, g_var_ready, g_root_ready, strip)
                    after(g_ln_step, base + G0_END - 1)
                    nc.vector.tensor_scalar(rows_of(s), strip, 1.0, None, ALU.mult).then_inc(g_ln_step, 1)
                    dve.wait_ge(g_xT_done, s + 1)
                with dve.Fori(0, NS) as s:
                    with dve.Fori(0, BODIES) as g:
                        for k in range(SLOTS):
                            dve.wait_ge(g_load[k], ((s + NS) * BODIES + g + 1) * 16)
                            for t in range(TI):
                                n = ((s * BODIES + g) * SLOTS + k) * TI + t
                                dve.wait_ge(g_used, n - 1 + G_CREDIT)
                                dve.wait_ge(g_ready, n + 1 + ONE)
                                nc.vector.scalar_tensor_tensor(
                                    junk[t % 2][:, 0:CJ], g_acc[:, t % GRING, :], 1.0, A[k][:, t, :], ALU.mult, ALU.mult,
                                    accum_out=part[:, t, bass.ds(g * SLOTS + k, 1)]).then_inc(g_used, 1)
                    dve.wait_ge(g_used, (s + 1) * NQ * TI + G_CREDIT)
                    base = s * G1_END + NS * G0_END
                    after(g_ln_step, base)
                    nc.vector.tensor_reduce(col[0][:, :], part, AXX, ALU.add).then_inc(g_ln_step, 1)
                    for k in range(4):
                        combine(k, g_ln_step, base + 1, rows_of(s), R_CONST)
                    dve.wait_ge(g_out_sent, (s + 1) * 16)
                    for k in range(NORM):
                        normalise(k, g_ln_step, base + 5, s + NS, g_var_ready, g_root_ready, y[:, :, :])
                    after(g_ln_step, base + G1_END)
                    dve.sem_inc(g_y_ready, 1)
            with dve.Else():
                def masks1(s, g, down, u):
                    dve.wait_ge(m1_used, (s * BODIES + g) * STEPS + u + 1)
                    unpack(STEPS - 1 - u, bits[:, bass.ds(s * BODIES + down, 1), :].rearrange("p g i -> p (g i)"),
                           mask[u % MASKS], m1_ready)

                def strip1(s, half):
                    for g in range(BODIES):
                        for u in range(STEPS):
                            masks1(s, g, BODIES - 1 - g, u)
                            for k in ENDS_AT.get(g * STEPS + u, ()):
                                finish1(k, s - 1, half)

                dve.wait_ge(ct_done, NS * NB + MASKS)
                for g in range(BODIES):
                    for u in range(STEPS):
                        masks1(0, g, BODIES - 1 - g, u)
                        for k in ENDS0_AT.get(g * STEPS + u, ()):
                            finish0(k, NS - 1)
                with dve.Fori(0, NS // 2 - 1) as pair:
                    for turn in (1, 2):
                        strip1(pair * 2 + turn, turn % 2)
                strip1(NS - 1, 1)
                for k in range(FINISH1):
                    finish1(k, NS - 1, 0)
            dve.nop()

        @block.tensor
        def _(pe):
            pe.sem_inc(ct_done, MASKS)
            pe.sem_inc(sup_done, WGT_CREDIT)
            pe.sem_inc(tile_done, LOAD_CREDIT)
            pe.sem_inc(m1_used, MASKS)
            pe.wait_ge(ident_ready, 1)

            def group_T(s, T, copied, x_in):
                if s * X_LOADS % NS == 0:
                    pe.wait_ge(x_in[s * X_LOADS // NS], 16)
                if s >= 2:
                    pe.wait_ge(copied, s - 1)
                for t in range(PAIRS):
                    b = s * TI + 2 * t
                    last = nc.tensor.transpose(word_half[s % 2][:, t * P:(t + 1) * P],
                                               x_all[:, b:b + 2, :].rearrange("p b d -> p (b d)"), ident[:, :])
                last.then_inc(T, 1)

            def groups_of_rows(x_in, w_ready, T, copied, sup, read):
                group_T(0, T, copied, x_in)
                pe.wait_ge(w_ready, 1)
                for s in range(NS):
                    if s + 1 < NS:
                        group_T(s + 1, T, copied, x_in)
                    pe.wait_ge(copied, s + 1)
                    if s >= 2:
                        pe.wait_ge(read, s - 1)
                    for t in range(PAIRS):
                        c0 = s % 2 * 512 + t * P
                        last = nc.tensor.matmul(banks[:, s % 2, t * P:(t + 1) * P], x_groupT[:, c0:c0 + P],
                                                w_pair[:, :], start=True, stop=True)
                    last.then_inc(sup, 1)

            groups_of_rows(x_in, w_ready_pair, grp_T, grp_Tcopied, grp_sup, pieces_ready)
            pe.wait_ge(const_done, 6)
            pe.wait_ge(fold_ready, 1)
            pe.wait_ge(bits_ready, STEPS)

            def tile_in(v, g):
                k, tj = v // TJ, TJ - 1 - v % TJ
                if v % TJ == 0:
                    pe.wait_ge(a_load[k], (g + 1) * 16)
                if v == 0:
                    pe.wait_ge(word_read, g + ONE)
                for t in range(TI):
                    last = nc.tensor.matmul(word[:, t * P:(t + 1) * P],
                                            A_high[k][:, t, 2 * tj * P + 1:2 * (tj + 1) * P:2], bit_ident[:, v, :],
                                            start=v == 0 and t % 4 == 0, stop=True, skip_group_check=True)
                last.then_inc(tile_done, 1)

            def zero_banks(first, n):
                for b in range(first, first + n):
                    nc.tensor.matmul(banks[:, b, :], zeros[:, 0:P], zeros[:, :], start=True, stop=True)

            def zero_count(c):
                return nc.tensor.matmul(count[c], zeros[:, 0:P], zeros[:, 0:HALF], start=True, stop=True)

            def zero_counts():
                for c in range(CHAINS):
                    zero_count(c)

            def counts(mask, c, table, start=False):
                return nc.tensor.matmul(count[c], table[:, :], mask[:, c * HALF:(c + 1) * HALF],
                                        start=start, stop=True, skip_group_check=True)

            def add_rows(block, c, weights, total, start=False):
                return nc.tensor.matmul(total[:, c, :], support[:, block, :], weights, start=start, stop=True,
                                        skip_group_check=True)

            def turn_back(k, turn):
                pe.wait_ge(acc_read, turn)
                for t in range(TI):
                    last = nc.tensor.matmul(turned[k][:, t, :], sums_sb[:, t * P:(t + 1) * P], fold[:, :],
                                            start=True, stop=True)
                last.then_inc(turned_ready, 1)

            def g_add_rows(block, c, lhs):
                for t in range(TH):
                    i = c * TH + t
                    last = nc.tensor.matmul(g_acc[:, i // 2, (i % 2) * G_PIECES:(i % 2 + 1) * G_PIECES],
                                            lhs[:, t * P:(t + 1) * P], g_support[:, block, :],
                                            start=False, stop=True, skip_group_check=True)
                return last

            def from_last(down, u):
                return down * STEPS + (STEPS - 1 - u)

            def count_ahead(n, u, c, start):
                if c == 0:
                    pe.wait_ge(m_ready, n + 1)
                counts(mask[u % MASKS], c, count_w, start).then_inc(v_ready, 1)

            def body0(s, g, down, first, end, final, groups_left):
                group = s * BODIES + g
                for u in range(STEPS):
                    n = group * STEPS + u
                    on, v = divmod(u + AHEAD, STEPS)
                    for c in range(CHAINS):
                        pe.wait_ge(w_ready, n * CHAINS + c + 1)
                        last_of_strip = end and not final and u == STEPS - 1
                        if last_of_strip and c == CHAINS - 1:
                            zero_count(c).then_inc(ct_done, 1)
                        elif not last_of_strip:
                            m = counts(mask[u % MASKS], c, carry_w)
                            if c == CHAINS - 1:
                                m.then_inc(ct_done, 1)
                        if not (final and u == STEPS - 1):
                            count_ahead(n + 1, u + 1, c, last_of_strip and c == 0)
                        if first and u == 0:
                            if c == 0:
                                tile_in(v, group + 1 + on)
                            continue
                        if first and u == 1 and c == 0:
                            pe.wait_ge(acc_read, s + ONE)
                            for b in range(CHAINS):
                                add_rows(from_last(down, 0), b, wgt[b][0][:, :], sums, True).then_inc(sup_done, 1)
                        add_rows(from_last(down, u), c, wgt[c][u % 2][:, :], sums).then_inc(sup_done, 1)
                        if c == (0 if v else 1) and on < groups_left:
                            tile_in(v, group + 1 + on)
                    if first and u == TURN_AT0:
                        turn_back(0, s + ONE)

            def strip0(s, last):
                body0(s, 0, BODIES - 1, True, False, False, 2)
                with pe.Fori(1, BODIES - 2 if last else BODIES - 1) as g:
                    body0(s, g, pe.snap(BODIES - 1 - g), False, False, False, 2)
                if last:
                    body0(s, BODIES - 2, 1, False, False, False, 1)
                    pe.wait_ge(odd_ready, 1)
                    pe.wait_ge(word_read, GROUPS + ONE)
                    nc.tensor.matmul(word[0:1, 0:1], odd_sum[:, :], ones[:, :], start=True,
                                     stop=True).then_inc(odd_total, 1)
                    body0(s, BODIES - 1, 0, False, True, True, 0)
                else:
                    body0(s, BODIES - 1, 0, False, True, False, 2)

            pe.wait_ge(grp_Tcopied, NS)
            for v in range(STEPS + AHEAD):
                tile_in(v % STEPS, v // STEPS)
            pe.wait_ge(pieces_ready, NS)
            for c in range(CHAINS):
                count_ahead(0, 0, c, True)
            with pe.Fori(0, NS - 1) as s:
                strip0(s, False)
            strip0(NS - 1, True)

            pe.wait_ge(flag_ready, 1)
            general = pe.value_load(flag[0:1, 0:1])
            with pe.If(general != 0):
                pe.sem_inc(g_ct_done, G_MASK_CREDIT)
                pe.sem_inc(g_tp_done, LOAD_CREDIT)
                pe.sem_inc(g_sup_done, WGT_CREDIT)
                pe.sem_inc(g_ready, ONE)
                turn_back(0, NS + ONE)
                pe.wait_ge(g_x_in, 16)
                groups_of_rows([g_x_in] * X_LOADS, g_w_ready_pair, g_T, g_Tcopied, g_sup, g_rest_ready)
                pe.wait_ge(g_pieces_ready, NS)
                with pe.Fori(0, NS) as s:
                    zero_counts()
                    pe.wait_ge(g_acc_read, s + ONE)
                    zero_banks(0, GRING)
                    with pe.Fori(0, BODIES) as g:
                        down = pe.snap(BODIES - 1 - g)
                        for u in range(STEPS):
                            k, tj = u // TJ, TJ - 1 - u % TJ
                            n = (s * BODIES + g) * STEPS + u
                            if u % TJ == 0:
                                pe.wait_ge(g_load[k], (s * BODIES + g + 1) * 16)
                            pe.wait_ge(g_m_ready, n + 1)
                            for t in range(TI):
                                last = nc.tensor.transpose(tp[u % 2][:, t * P:(t + 1) * P],
                                                           A_high[k][:, t, 2 * tj * P + 1:2 * (tj + 1) * P:2],
                                                           ident_b[:, :])
                            last.then_inc(g_tp_done, 1)
                            pe.wait_ge(g_m_ready, n + 1 + G_MASK_CREDIT)
                            for c in range(CHAINS):
                                counts(mask[u % 2], c, count_w).then_inc(g_v_ready, 1)
                            for c in range(CHAINS):
                                pe.wait_ge(g_w_ready, n * CHAINS + c + 1)
                                m = counts(mask[u % 2], c, carry_w)
                                if c == CHAINS - 1:
                                    m.then_inc(g_ct_done, 1)
                                g_add_rows(from_last(down, u), c, wgt[c][u % 2]).then_inc(g_sup_done, 1)
                    pe.wait_ge(g_ln_step, s * G0_END + G0_END - 1 + ONE)
                    pe.wait_ge(g_m_ready, (s + 1) * NB + G_MASK_CREDIT)
                    for t in range(TI):
                        last = nc.tensor.transpose(word_half[t // 4][:, (t % 4) * P:(t % 4 + 1) * P],
                                                   strip_pad[:, t, :], ident[:, :])
                    last.then_inc(g_xT_done, 1)
                    pe.wait_ge(g_xT_copied, 2 * (s + 1))
                with pe.Fori(0, NS) as s:
                    pe.wait_ge(g_xi_ready, s + 1)
                    pe.sem_inc(product_turn, 1)
                    with pe.Fori(0, BODIES) as g:
                        down = pe.snap(BODIES - 1 - g)
                        for k in range(SLOTS):
                            j0 = down * (SLOTS * CJ) + (SLOTS - 1 - k) * CJ
                            for t in range(TI):
                                n = ((s * BODIES + g) * SLOTS + k) * TI + t
                                pe.wait_ge(g_used, n + 1 + G_CREDIT - GRING)
                                pe.sem_inc(product_turn, 1)
                                nc.tensor.matmul(g_acc[:, t % GRING, :], x_groupT[:, t * P:(t + 1) * P],
                                                 xT[:, bass.ds(j0, CJ)], start=True, stop=True).then_inc(g_ready, 1)
            with pe.Else():
                def body1(s, g, turn, first):
                    for u in range(STEPS):
                        if u % TI == 0:
                            pe.wait_ge(pieces_ready, g * (STEPS // TI) + u // TI + 1 + NS)
                        pe.wait_ge(m1_ready, (s * BODIES + g) * STEPS + u + 1)
                        if u == 0:
                            pe.sem_inc(product_turn, 1)
                        for c in range(CHAINS):
                            last = add_rows(g * STEPS + u, c, mask[u % MASKS][:, c * HALF:(c + 1) * HALF].bitcast(F16),
                                            sums1[turn], first and u == 0)
                        last.then_inc(m1_used, 1)
                        if first and u == TURN_AT1:
                            turn_back(turn, s + NS + ONE)

                with pe.Fori(0, NS // 2) as pair:
                    for turn in range(2):
                        s = pair * 2 + turn
                        pe.wait_ge(acc_read, s + NS)
                        body1(s, 0, turn, True)
                        with pe.Fori(1, BODIES) as g:
                            body1(s, g, turn, False)
                turn_back(0, 2 * NS + ONE)
            pe.nop()


_INS = ['x', 'adj', 'L0_gnn_weight', 'L0_gnn_bias']
_OUTS = [((8192, 64), 'float32')]


def kernel(**inputs):
    import numpy as _np
    import concourse.bacc as _bacc
    from concourse import mybir as _mybir
    from concourse.bass_utils import run_bass_kernel_spmd as _run

    nc = _bacc.Bacc("TRN2", target_bir_lowering=False, num_devices=1)
    arrays, args = {}, []
    for name in _INS:
        a = _np.ascontiguousarray(inputs[name])
        arrays[f"in_{name}_dram"] = a
        args.append(nc.dram_tensor(f"in_{name}_dram", a.shape, _mybir.dt.from_np(a.dtype), kind="ExternalInput").ap())
    for i, (shape, dtype) in enumerate(_OUTS):
        dt = _mybir.dt.from_np(_np.dtype(dtype))
        args.append(nc.dram_tensor(f"out_{i}_dram", shape, dt, kind="ExternalOutput").ap())
    adj_resnorm_kernel(nc, *args)
    r = _run(nc, [arrays], core_ids=[0])
    got = tuple(r.results[0][f"out_{i}_dram"] for i in range(len(_OUTS)))
    return got[0]
```
